# Optimizing a Trainium2 kernel written in Bass

```python
import numpy as np
import jax
import jax.numpy as jnp

def _softmax(x, axis=-1):
    return jax.nn.softmax(x, axis=axis)

def _gelu(x):
    return jax.nn.gelu(x, approximate=True)

def _silu(x):
    return jax.nn.silu(x)

def _sigmoid(x):
    return jax.nn.sigmoid(x)

def _layernorm(x, axis=-1, eps=1e-05):
    m = jnp.mean(x, axis=axis, keepdims=True)
    v = jnp.var(x, axis=axis, keepdims=True)
    return (x - m) / jnp.sqrt(v + eps)

def _scatter_add(tgt, idx, src, axis=0):
    return tgt.at[idx].add(src)

def _segment_sum(src, seg, n):
    return jax.ops.segment_sum(src, seg, n)
kernel_name = 'mk_gnn_resnorm_d4_gnn_r8_3a257c'

def setup_inputs(seed: int=0):
    np.random.seed(seed)
    _w = jnp.asarray

    def _rec_inputs():
        import jax
        import jax.numpy as jnp
        _gk = jax.random.key(seed)
        x = -0.000202 + 1 * jax.random.normal(jax.random.fold_in(_gk, 1), (12500, 64), jnp.float32)
        src = jax.random.randint(jax.random.fold_in(_gk, 2), (200000,), 0, 12500, jnp.int32)
        dst = jax.random.randint(jax.random.fold_in(_gk, 3), (200000,), 0, 12500, jnp.int32)
        _o = jnp.argsort(dst, stable=True)
        src = src[_o]
        dst = dst[_o]
        edge_attr_4 = jax.random.uniform(jax.random.fold_in(_gk, 12), (200000, 4), jnp.float32, 0.0, 1)
        edge_weight = jax.random.uniform(jax.random.fold_in(_gk, 14), (200000,), jnp.float32, 0.0, 0.999999)
        node_vec = jax.random.uniform(jax.random.fold_in(_gk, 15), (12500,), jnp.float32, 0.0, 31.9963)
        return (x, src, dst, edge_attr_4, edge_weight, node_vec)
    x, src, dst, edge_attr_4, edge_weight, node_vec = _rec_inputs()

    def _L0_gnn_setup():
        import jax, jax.numpy as jnp
        import numpy as np
        N_NODES = 12500
        N_EDGES = 200000
        D = 64
        H = 128
        key = jax.random.key(seed)
        k = jax.random.split(key, 8)
        feat = jax.random.normal(k[0], (N_NODES, D), dtype=jnp.float32)
        edge_src = jax.random.randint(k[1], (N_EDGES,), 0, N_NODES, dtype=jnp.int32)
        edge_dst = jax.random.randint(k[2], (N_EDGES,), 0, N_NODES, dtype=jnp.int32)
        W1 = jax.random.normal(k[3], (D, H), dtype=jnp.float32) * (1.0 / np.sqrt(D))
        b1 = jnp.zeros((H,), dtype=jnp.float32)
        W2 = jax.random.normal(k[4], (H, D), dtype=jnp.float32) * (1.0 / np.sqrt(H))
        b2 = jnp.zeros((D,), dtype=jnp.float32)
        eps = jnp.zeros((1,), dtype=jnp.float32)
        return {'feat': feat, 'edge_src': edge_src, 'edge_dst': edge_dst, 'W1': W1, 'b1': b1, 'W2': W2, 'b2': b2, 'eps': eps}
    _L0_gnn_all = _L0_gnn_setup()
    _L0_gnn_in = {k: v for k, v in _L0_gnn_all.items() if k in ('W1', 'b1', 'W2', 'b2', 'eps')}
    del _L0_gnn_all

    def _L1_gnn_setup():
        import jax, jax.numpy as jnp
        import numpy as np
        N = 6250
        E = 100000
        C = 64
        key = jax.random.key(seed)
        ks = jax.random.split(key, 16)
        s = 0.05
        x = jax.random.normal(ks[0], (N, C), jnp.float32)
        edge_attr = jax.random.uniform(ks[1], (E, 4), dtype=jnp.float32)
        edge_index = jax.random.randint(ks[2], (2, E), 0, N)
        deg_hist = jax.random.uniform(ks[3], (N,), dtype=jnp.float32) * 32.0
        W = jax.random.normal(ks[4], (C, C), jnp.float32) * s
        We = jax.random.normal(ks[5], (3, C), jnp.float32) * s
        be = jnp.zeros((C,), jnp.float32)
        Wpre = jax.random.normal(ks[6], (3 * C, C), jnp.float32) * s
        bpre = jnp.zeros((C,), jnp.float32)
        A_S = 4 * 3
        Wpost = jax.random.normal(ks[7], ((A_S + 1) * C, C), jnp.float32) * s
        bpost = jnp.zeros((C,), jnp.float32)
        Wih = jax.random.normal(ks[8], (C, 3 * C), jnp.float32) * s
        bih = jnp.zeros((3 * C,), jnp.float32)
        Whh = jax.random.normal(ks[9], (C, 3 * C), jnp.float32) * s
        bhh = jnp.zeros((3 * C,), jnp.float32)
        return dict(x=x, edge_attr=edge_attr, deg_hist=deg_hist, W=W, We=We, be=be, Wpre=Wpre, bpre=bpre, Wpost=Wpost, bpost=bpost, Wih=Wih, bih=bih, Whh=Whh, bhh=bhh, edge_index=edge_index)
    _L1_gnn_all = _L1_gnn_setup()
    _L1_gnn_in = {k: v for k, v in _L1_gnn_all.items() if k in ('W', 'We', 'be', 'Wpre', 'bpre', 'Wpost', 'bpost', 'Wih', 'bih', 'Whh', 'bhh')}
    del _L1_gnn_all

    def _L2_gnn_setup():
        import jax, jax.numpy as jnp
        import numpy as np
        N_NODES = 6250
        N_EDGES = 200000
        IN_CH = 64
        OUT_CH = 64
        key = jax.random.key(seed)
        k1, k2, k3, k4, k5 = jax.random.split(key, 5)
        x = jax.random.normal(k1, (N_NODES, IN_CH), dtype=jnp.float32)
        edge_index = jax.random.randint(k2, (2, N_EDGES), 0, N_NODES, dtype=jnp.int64)
        edge_attr = jax.random.uniform(k3, (N_EDGES,), dtype=jnp.float32)
        bound = 1.0 / np.sqrt(2 * IN_CH)
        weight = jax.random.uniform(k4, (2 * IN_CH, OUT_CH), dtype=jnp.float32, minval=-bound, maxval=bound)
        bias = jax.random.uniform(k5, (OUT_CH,), dtype=jnp.float32, minval=-bound, maxval=bound)
        return {'x': x, 'edge_index': edge_index, 'edge_attr': edge_attr, 'weight': weight, 'bias': bias}
    _L2_gnn_all = _L2_gnn_setup()
    _L2_gnn_in = {k: v for k, v in _L2_gnn_all.items() if k in ('weight', 'bias')}
    del _L2_gnn_all

    def _L3_gnn_setup():
        import jax, jax.numpy as jnp
        import numpy as np
        N_NODES = 12500
        N_EDGES = 200000
        D_FEAT = 64
        D_OUT = 64
        key = jax.random.key(seed)
        k1, k2, k3, k4, k5 = jax.random.split(key, 5)
        node_features = jax.random.normal(k1, (N_NODES, D_FEAT), dtype=jnp.float32)
        edge_row = jax.random.randint(k2, (N_EDGES,), 0, N_NODES)
        edge_col = jax.random.randint(k3, (N_EDGES,), 0, N_NODES)
        edge_vals = jax.random.uniform(k4, (N_EDGES,), dtype=jnp.float32)
        W = jax.random.normal(k5, (D_FEAT, D_OUT), dtype=jnp.float32) * 0.05
        b = jnp.zeros((D_OUT,), dtype=jnp.float32)
        return {'node_features': node_features, 'edge_vals': edge_vals, 'W': W, 'b': b, 'edge_row': edge_row, 'edge_col': edge_col}
    _L3_gnn_all = _L3_gnn_setup()
    _L3_gnn_in = {k: v for k, v in _L3_gnn_all.items() if k in ('W', 'b')}
    del _L3_gnn_all
    return {'x': x, 'src': src, 'dst': dst, 'edge_attr_4': edge_attr_4, 'edge_weight': edge_weight, 'node_vec': node_vec, 'L0_gnn_W1': _L0_gnn_in['W1'], 'L0_gnn_b1': _L0_gnn_in['b1'], 'L0_gnn_W2': _L0_gnn_in['W2'], 'L0_gnn_b2': _L0_gnn_in['b2'], 'L0_gnn_eps': _L0_gnn_in['eps'], 'L1_gnn_W': _L1_gnn_in['W'], 'L1_gnn_We': _L1_gnn_in['We'], 'L1_gnn_be': _L1_gnn_in['be'], 'L1_gnn_Wpre': _L1_gnn_in['Wpre'], 'L1_gnn_bpre': _L1_gnn_in['bpre'], 'L1_gnn_Wpost': _L1_gnn_in['Wpost'], 'L1_gnn_bpost': _L1_gnn_in['bpost'], 'L1_gnn_Wih': _L1_gnn_in['Wih'], 'L1_gnn_bih': _L1_gnn_in['bih'], 'L1_gnn_Whh': _L1_gnn_in['Whh'], 'L1_gnn_bhh': _L1_gnn_in['bhh'], 'L2_gnn_weight': _L2_gnn_in['weight'], 'L2_gnn_bias': _L2_gnn_in['bias'], 'L3_gnn_W': _L3_gnn_in['W'], 'L3_gnn_b': _L3_gnn_in['b']}

def reference(x, src, dst, edge_attr_4, edge_weight, node_vec, L0_gnn_W1, L0_gnn_b1, L0_gnn_W2, L0_gnn_b2, L0_gnn_eps, L1_gnn_W, L1_gnn_We, L1_gnn_be, L1_gnn_Wpre, L1_gnn_bpre, L1_gnn_Wpost, L1_gnn_bpost, L1_gnn_Wih, L1_gnn_bih, L1_gnn_Whh, L1_gnn_bhh, L2_gnn_weight, L2_gnn_bias, L3_gnn_W, L3_gnn_b):
    import jax
    import jax.numpy as jnp

    def _L0_gnn_ref(feat, edge_src, edge_dst, W1, b1, W2, b2, eps):
        import jax, jax.numpy as jnp
        import numpy as np
        N_NODES = 12500
        N_EDGES = 200000
        D = 64
        H = 128
        neigh = jax.ops.segment_sum(feat[edge_src], edge_dst, num_segments=N_NODES)
        h = (1.0 + eps[0]) * feat + neigh
        h = jnp.maximum(h @ W1 + b1, 0.0) @ W2 + b2
        return h

    def _L1_gnn_ref(x, edge_attr, deg_hist, W, We, be, Wpre, bpre, Wpost, bpost, Wih, bih, Whh, bhh, edge_index):
        import jax, jax.numpy as jnp
        import numpy as np
        N = 6250
        E = 100000
        C = 64
        n_nodes = x.shape[0]
        m = x @ W
        src, dst = (edge_index[0], edge_index[1])
        ew = edge_attr[:, 3:4]
        ea = edge_attr[:, :3] @ We + be
        xi = ew * m[dst]
        xj = ew * m[src]
        ea = ew * ea
        h = jnp.concatenate([xi, xj, ea], axis=-1) @ Wpre + bpre
        ones = jnp.ones((h.shape[0],), h.dtype)
        cnt = jax.ops.segment_sum(ones, dst, num_segments=n_nodes)
        safe = jnp.maximum(cnt, 1.0)[:, None]
        s1 = jax.ops.segment_sum(h, dst, num_segments=n_nodes)
        s2 = jax.ops.segment_sum(h * h, dst, num_segments=n_nodes)
        mean = s1 / safe
        mean_sq = s2 / safe
        std = jnp.sqrt(jax.nn.relu(mean_sq - mean * mean) + 1e-05)
        has = (cnt > 0)[:, None]
        mn = jnp.where(has, jax.ops.segment_min(h, dst, num_segments=n_nodes), 0.0)
        mx = jnp.where(has, jax.ops.segment_max(h, dst, num_segments=n_nodes), 0.0)
        agg = jnp.concatenate([mean, mn, mx, std], axis=-1)
        deg = jnp.maximum(cnt, 1.0)[:, None]
        avg_log = jnp.mean(jnp.log(deg_hist + 1.0))
        logd = jnp.log(deg + 1.0)
        o1 = agg
        o2 = o1 * (logd / avg_log)
        o3 = o2 * (avg_log / logd)
        out = jnp.concatenate([o1, o2, o3], axis=-1)
        out = jnp.concatenate([m, out], axis=-1) @ Wpost + bpost
        gi = out @ Wih + bih
        gh = x @ Whh + bhh
        ir, iz, i_n = jnp.split(gi, 3, axis=-1)
        hr, hz, h_n = jnp.split(gh, 3, axis=-1)
        r = jax.nn.sigmoid(ir + hr)
        z = jax.nn.sigmoid(iz + hz)
        n = jnp.tanh(i_n + r * h_n)
        return (1.0 - z) * n + z * x

    def _L2_gnn_ref(x, edge_index, edge_attr, weight, bias):
        import jax, jax.numpy as jnp
        import numpy as np
        N_NODES = 6250
        N_EDGES = 200000
        IN_CH = 64
        OUT_CH = 64
        row, col = (edge_index[0], edge_index[1])
        num_node = x.shape[0]
        alpha = jnp.concatenate([x[row], x[col]], axis=-1) @ weight
        alpha = edge_attr[:, None] * alpha
        sums = jax.ops.segment_sum(alpha, row, num_segments=num_node)
        counts = jax.ops.segment_sum(jnp.ones((row.shape[0],), dtype=alpha.dtype), row, num_segments=num_node)
        out = sums / jnp.maximum(counts, 1.0)[:, None]
        return out + bias

    def _L3_gnn_ref(node_features, edge_vals, W, b, edge_row, edge_col):
        import jax, jax.numpy as jnp
        import numpy as np
        N_NODES = 12500
        N_EDGES = 200000
        D_FEAT = 64
        D_OUT = 64
        gathered = node_features[edge_col] * edge_vals[:, None]
        agg = jax.ops.segment_sum(gathered, edge_row, num_segments=N_NODES)
        return agg @ W + b
    edge_index = jnp.stack([src, dst])
    x = _layernorm(x + _L0_gnn_ref(x, src, dst, L0_gnn_W1, L0_gnn_b1, L0_gnn_W2, L0_gnn_b2, L0_gnn_eps), axis=-1)
    x = _layernorm(x + _L1_gnn_ref(x, edge_attr_4, node_vec, L1_gnn_W, L1_gnn_We, L1_gnn_be, L1_gnn_Wpre, L1_gnn_bpre, L1_gnn_Wpost, L1_gnn_bpost, L1_gnn_Wih, L1_gnn_bih, L1_gnn_Whh, L1_gnn_bhh, edge_index), axis=-1)
    x = _layernorm(x + _L2_gnn_ref(x, edge_index, edge_weight, L2_gnn_weight, L2_gnn_bias), axis=-1)
    x = _layernorm(x + _L3_gnn_ref(x, edge_weight, L3_gnn_W, L3_gnn_b, src, dst), axis=-1)
    return x

_drawn_inputs = setup_inputs


def setup_inputs(seed=0):
    import zlib

    import numpy as np

    out = dict(_drawn_inputs(seed))
    spreads = {'L0_gnn_b1': (0.0, 0.307),
     'L0_gnn_b2': (0.0, 0.1),
     'L1_gnn_be': (0.0, 0.8),
     'L1_gnn_bpre': (0.0, 1.676),
     'L1_gnn_bpost': (0.0, 2.0),
     'L1_gnn_bih': (0.0, 0.8),
     'L1_gnn_bhh': (0.0, 1.28),
     'L3_gnn_b': (0.0, 0.1)}
    factors = {'edge_attr_4': 8.0, 'node_vec': 8.0, 'L1_gnn_We': 8.0, 'L1_gnn_Wpre': 2.949}
    for name, (base, spread) in spreads.items():
        noise = np.random.default_rng([zlib.crc32(name.encode()), seed]).standard_normal(out[name].shape)
        drawn = base * np.exp(spread * noise) if base else spread * noise
        out[name] = jnp.asarray(drawn.astype(out[name].dtype))
    for name, factor in factors.items():
        out[name] = (out[name] * factor).astype(out[name].dtype)
    return out
```

```python
from contextlib import ExitStack

import concourse.bass as bass
from concourse import mybir

F32 = mybir.dt.float32
BF16 = mybir.dt.bfloat16
I32 = mybir.dt.int32
U8 = mybir.dt.uint8
ALU = mybir.AluOpType
ACT = mybir.ActivationFunctionType
AX_X = mybir.AxisListType.X

P = 128
N = 12500
E = 200000
C = 64
C1 = C + 1
HID = 128
NT = -(-N // P)
NTP = 100
DUMMY = NT
ET = -(-E // P)
B4 = 4
ROUND = 8
STEPS = -(-(ET + NT - 1) // (B4 * ROUND)) * B4 * ROUND
CH = STEPS // P
NB = STEPS // B4
ROUNDS = NB // ROUND
FULL = E // P
TAIL = E - FULL * P
FULLCH = FULL // P
REST = FULL - FULLCH * P
FAR = 1 << 20
NEG = -3.0e38
K = 8
F = C + 2
NF = 9
SRC, DST, FIRST, LAST, EW, W, EA = 0, 1, 2, 3, 4, 5, 6
EPS = 1e-5
GRP = 4
GROUPS = NTP // GRP
ZERO = 600

INS = ['x', 'src', 'dst', 'edge_attr_4', 'edge_weight', 'node_vec', 'L0_gnn_W1', 'L0_gnn_b1', 'L0_gnn_W2',
       'L0_gnn_b2', 'L0_gnn_eps', 'L1_gnn_W', 'L1_gnn_We', 'L1_gnn_be', 'L1_gnn_Wpre', 'L1_gnn_bpre',
       'L1_gnn_Wpost', 'L1_gnn_bpost', 'L1_gnn_Wih', 'L1_gnn_bih', 'L1_gnn_Whh', 'L1_gnn_bhh',
       'L2_gnn_weight', 'L2_gnn_bias', 'L3_gnn_W', 'L3_gnn_b']


class Shared:
    pass


class Carver:

    def __init__(self, tensor, at=0):
        self.t, self.at = tensor, at

    def f32(self, n):
        v = self.t[:, self.at:self.at + n]
        self.at += n
        assert self.at <= self.t.shape[1], (self.at, self.t.shape)
        return v

    def bf16(self, n):
        return self.f32(n // 2).bitcast(BF16)

    def i32(self, n):
        return self.f32(n).bitcast(I32)


def rounds(eng, tick, behind):
    for b in range(ROUND):
        tick(0, b)
    with eng.Fori(1, ROUNDS) as r:
        base = r * ROUND
        for b in range(ROUND):
            tick(base, b)
    for b in range(behind):
        tick(NB, b)


def live(base, b, lag):
    return not isinstance(base, int) or 0 <= base + b - lag < NB


def wait(eng, sem, value):
    if not isinstance(value, int) or value > 0:
        eng.wait_ge(sem, value)


def pipeline(eng, tick, depth):
    for g in range(depth):
        tick(g)
    with eng.Fori(depth, GROUPS) as g:
        tick(g)
    for g in range(GROUPS, GROUPS + depth):
        tick(g)


def group_live(g, lag):
    return not isinstance(g, int) or 0 <= g - lag < GROUPS


def chain(eng, sem):
    n = [0]

    def done(op):
        n[0] += 1
        op.then_inc(sem, 1)
        eng.wait_ge(sem, n[0])
    return done


def prepare(nc, s, A):
    ar = Carver(s.arena)
    rows = ar.f32(CH * NF * P)
    rows_v = rows.rearrange("p (c f e) -> p c f e", c=CH, f=NF)
    scratch_at = ar.at
    raw_attr, raw_src, raw_dst = ar.f32(CH * 4 * P), ar.i32(CH * P), ar.i32(CH * P)
    raw_attr_v, raw_src_v, raw_dst_v = (t.rearrange("p (c e) -> p c e", c=CH) for t in (raw_attr, raw_src, raw_dst))
    wk = Carver(s.work, s.pass0_at)
    before_i, behind_i, last_tile_i, edge_tile_i, node_tile_i = (wk.i32(CH) for _ in range(5))
    before_f, behind_f, ends, edge_tile, node_tile_f, node_base, tile_no = (wk.f32(CH) for _ in range(7))
    ends_row, less = wk.f32(CH * P), wk.f32(CH * P)
    dummy_row, ones_edges, eps0 = wk.f32(P), wk.f32(P), wk.f32(1)
    tile_row_i = less.bitcast(I32)

    raw_clean, raw_loaded, consts, fields, edge_stored, by_step = (
        s.sem(n) for n in ("raw_clean", "raw_loaded", "consts", "fields", "edge_stored", "by_step"))
    ends_ready, ends_turned, step_work, tiles_ready, tiles_stored, tiles_loaded = (
        s.sem(n) for n in ("ends_ready", "ends_turned", "step_work", "tiles_ready", "tiles_stored", "tiles_loaded"))
    x_clean, x_loaded, eps_loaded = (s.sem(n) for n in ("x_clean", "x_loaded", "eps_loaded"))
    whole = FULLCH * P * P
    n_loads = 3 * 4 + 6

    def load_edges(eng, to, of, width):
        w = P * width
        eng.dma_start(to[:, 0:FULLCH, :], of[0:whole * width].rearrange("(c p e) -> p c e", p=P, e=w)).then_inc(raw_loaded, 16)
        eng.dma_start(to[0:REST, FULLCH, :], of[whole * width:FULL * w].rearrange("(p e) -> p e", e=w)).then_inc(raw_loaded, 16)
        eng.dma_start(to[REST:REST + 1, FULLCH, 0:TAIL * width],
                      of[FULL * w:E * width].rearrange("(p e) -> p e", p=1)).then_inc(raw_loaded, 16)

    with nc.Block() as block:
        @block.sync
        def _(sp):
            sp.wait_ge(raw_clean, 6)
            load_edges(sp, raw_dst_v, A["dst"], 1)
            load_edges(sp, raw_src_v, A["src"], 1)
            load_edges(sp, rows_v[:, :, W, :], A["edge_weight"], 1)
            load_edges(sp, raw_attr_v, A["edge_attr_4"].rearrange("e f -> (e f)"), 4)
            with nc.allow_non_contiguous_dma(reason="one number for each tile of 128 edges"):
                def one_per_tile(first, tiles):
                    return A["dst"][first:first + (tiles - 1) * P + 1:P]
                sp.dma_start(before_i[1:P, 0:1], one_per_tile(P - 1, P - 1).unsqueeze(1)).then_inc(raw_loaded, 16)
                sp.dma_start(before_i[:, 1:FULLCH], one_per_tile(P * P - 1, (FULLCH - 1) * P)
                             .rearrange("(c p) -> p c", p=P)).then_inc(raw_loaded, 16)
                sp.dma_start(before_i[0:REST + 1, FULLCH:CH], one_per_tile(whole - 1, REST + 1).unsqueeze(1)).then_inc(raw_loaded, 16)
                sp.dma_start(behind_i[:, 0:FULLCH], one_per_tile(P, FULLCH * P)
                             .rearrange("(c p) -> p c", p=P)).then_inc(raw_loaded, 16)
                sp.dma_start(behind_i[0:REST, FULLCH:CH], one_per_tile(whole + P, REST).unsqueeze(1)).then_inc(raw_loaded, 16)
                sp.dma_start(eps0, A["L0_gnn_eps"].partition_broadcast(P)).then_inc(raw_loaded, 16)
            sp.wait_ge(fields, 1)
            sp.dma_start(s.edge_rows.rearrange("(c p) f -> p c f", p=P),
                         rows.rearrange("p (c f) -> p c f", c=CH)).then_inc(edge_stored, 16)
            sp.wait_ge(tiles_ready, 1)
            with nc.allow_non_contiguous_dma(reason="one number for each step"):
                sp.dma_start(s.tile_list.rearrange("(c p) -> p c", p=P), node_tile_i).then_inc(tiles_stored, 16)
            sp.wait_ge(tiles_stored, 16)
            sp.dma_start(tile_row_i[0:1, :], s.tile_list.rearrange("(a n) -> a n", a=1)).then_inc(tiles_loaded, 16)
            sp.wait_ge(tiles_loaded, 16)
            sp.wait_ge(edge_stored, 16)

        @block.scalar
        def _(act):
            act.wait_ge(x_clean, 2)
            act.dma_start(s.Xv[:, 0:NT - 1, 0:C], A["x"][0:(NT - 1) * P, :].rearrange("(j p) f -> p j f", p=P)).then_inc(x_loaded, 16)
            act.dma_start(s.Xv[0:N - (NT - 1) * P, NT - 1, 0:C], A["x"][(NT - 1) * P:N, :]).then_inc(x_loaded, 16)
            act.wait_ge(x_loaded, 32)

        @block.gpsimd
        def _(pool):
            def numbers(to, pattern, base, by_partition):
                nc.gpsimd.iota(to, pattern=pattern, base=base, channel_multiplier=by_partition,
                               allow_small_or_imprecise_dtypes=True).then_inc(consts, 1)
            numbers(s.iota_row[:, :], [[1, P]], 0, 0)
            numbers(s.iota_col[:, :], [[0, 1]], 0, 1)
            numbers(tile_no, [[P, CH]], 0, 1)
            numbers(dummy_row, [[NTP, P]], DUMMY, 0)
            numbers(s.dummy_col[:, :], [[0, 1]], DUMMY, NTP)
            nc.gpsimd.memset(s.ident[:, :], 1.0).then_inc(consts, 1)
            pool.wait_ge(consts, 6)
            nc.gpsimd.affine_select(out=s.ident[:, :], in_=s.ident[:, :], compare_op=ALU.is_equal, fill=0.0,
                                    base=0, pattern=[[-1, P]], channel_multiplier=1).then_inc(consts, 1)
            pool.wait_ge(edge_stored, 16)
            pool.wait_ge(tiles_ready, 1)
            for c in range(CH):
                pool.indirect_dma_start(rows[:, c * NF * P:(c + 1) * NF * P], None, s.edge_rows,
                                        bass.IndirectOffsetOnAxis(ap=edge_tile_i[:, c:c + 1], axis=0)).then_inc(by_step, 16)
            pool.wait_ge(by_step, 16 * CH)

        @block.tensor
        def _(pe):
            pe.wait_ge(consts, 7)
            pe.wait_ge(ends_ready, 1)
            for c in range(CH):
                pe.transpose(s.psum[:, c * P:(c + 1) * P], ends[:, c:c + 1].broadcast_to((P, P)),
                             s.ident[:, :]).then_inc(ends_turned, 1)

        @block.vector
        def _(dve):
            done = chain(dve, step_work)
            v = nc.vector
            v.memset(raw_src_v[:, CH - 1, :], 0).then_inc(raw_clean, 1)
            v.memset(raw_dst_v[:, CH - 1, :], FAR).then_inc(raw_clean, 1)
            v.memset(raw_attr_v[:, CH - 1, :], 0.0).then_inc(raw_clean, 1)
            v.memset(rows_v[:, CH - 1, W, :], 0.0).then_inc(raw_clean, 1)
            v.memset(before_i, -1).then_inc(raw_clean, 1)
            v.memset(behind_i, FAR).then_inc(raw_clean, 1)
            v.memset(s.Xv[:, :, 0:C], 0.0).then_inc(x_clean, 1)
            v.memset(s.Xv[:, :, C:C1], 1.0).then_inc(x_clean, 1)
            v.memset(s.zeros, 0.0)
            v.memset(s.ones_row[:, :], 1.0)
            v.memset(ones_edges, 1.0)
            done(v.memset(s.eps_col[:, :], EPS))
            dve.wait_ge(raw_loaded, 16 * n_loads)
            done(v.tensor_scalar(s.one_eps[:, :], eps0, 1.0, None, ALU.add))
            done(v.tensor_copy(rows_v[:, :, DST, :], raw_dst_v))
            v.tensor_copy(rows_v[:, :, SRC, :], raw_src_v)
            v.tensor_copy(before_f, before_i)
            done(v.tensor_copy(behind_f, behind_i))
            D = rows_v[:, :, DST, :]
            v.tensor_tensor(rows_v[:, :, FIRST, 1:P], D[:, :, 1:P], D[:, :, 0:P - 1], ALU.not_equal)
            v.tensor_tensor(rows_v[:, :, FIRST, 0], D[:, :, 0], before_f, ALU.not_equal)
            v.tensor_tensor(rows_v[:, :, LAST, 0:P - 1], D[:, :, 1:P], D[:, :, 0:P - 1], ALU.not_equal)
            v.tensor_tensor(rows_v[:, :, LAST, P - 1], D[:, :, P - 1], behind_f, ALU.not_equal)
            by_edge = raw_attr.rearrange("p (c e f) -> p c e f", c=CH, f=4)
            v.tensor_copy(rows_v[:, :, EW, :], by_edge[:, :, :, 3])
            for f in range(3):
                last = v.tensor_copy(rows_v[:, :, EA + f, :], by_edge[:, :, :, f])
            done(last)
            v.engine_nop().then_inc(fields, 1)
            done(v.tensor_scalar(last_tile_i, raw_dst_v[:, :, P - 1], 7, None, ALU.logical_shift_right))
            done(v.tensor_copy(ends, last_tile_i))
            dve.wait_ge(consts, 7)
            done(v.tensor_tensor(ends, ends, tile_no, ALU.add))
            v.engine_nop().then_inc(ends_ready, 1)
            dve.wait_ge(ends_turned, CH)
            done(v.tensor_copy(ends_row, s.psum[:, 0:CH * P]))
            for c in range(CH):
                done(v.tensor_scalar(less, ends_row, tile_no[:, c:c + 1], None, ALU.is_lt))
                done(v.tensor_reduce(edge_tile[:, c:c + 1], less, AX_X, ALU.add))
            done(v.tensor_tensor(node_tile_f, tile_no, edge_tile, ALU.subtract))
            done(v.tensor_scalar(node_base, node_tile_f, float(P), None, ALU.mult))
            done(v.tensor_scalar(node_tile_f, node_tile_f, float(NT - 1), None, ALU.min))
            v.tensor_copy(node_tile_i, node_tile_f)
            done(v.tensor_copy(edge_tile_i, edge_tile))
            v.engine_nop().then_inc(tiles_ready, 1)
            dve.wait_ge(tiles_loaded, 16)
            done(v.tensor_copy(s.node_tile[:, :], tile_row_i[0:1, :]))

    ar = Carver(s.arena, scratch_at)
    src_i, low, high = ar.i32(CH * P), ar.i32(CH * P), ar.i32(CH * P)
    table_row, member, target = ar.f32(CH * P), ar.f32(CH * P), ar.f32(CH * P)
    reset = src_i.bitcast(BF16)[:, 0:CH * P]
    row3 = lambda t: t.rearrange("p (c e) -> p c e", c=CH)
    row_work, resets_ready, rows_out, columns = (s.sem(n) for n in ("row_work", "resets_ready", "rows_out", "columns"))
    field_ready, turned = s.sem("field_ready"), s.sem("turned")
    cols = [(rows_v[:, :, SRC, :], s.feature_row), (row3(table_row), s.message_row[:, :]), (row3(target), s.target_col),
            (rows_v[:, :, DST, :], s.rel_col[:, :]), (rows_v[:, :, LAST, :], s.last_col[:, :]),
            (rows_v[:, :, EW, :], s.ew_col[:, :]), (rows_v[:, :, W, :], s.weight_col)]
    parts = [(a, min(B4, CH - a)) for a in range(0, CH, B4)]

    with nc.Block() as block:
        @block.vector
        def _(dve):
            done = chain(dve, row_work)
            v = nc.vector
            R = rows_v
            by_row = lambda t: t.unsqueeze(1).broadcast_to((P, CH, P))
            v.tensor_tensor(R[:, :, DST, :], R[:, :, DST, :], node_base.unsqueeze(2).broadcast_to((P, CH, P)), ALU.subtract)
            done(v.tensor_copy(row3(src_i), R[:, :, SRC, :]))
            v.tensor_scalar(low, src_i, P - 1, None, ALU.bitwise_and)
            done(v.tensor_scalar(high, src_i, 7, None, ALU.logical_shift_right))
            v.tensor_scalar(row3(reset), R[:, :, FIRST, :], NEG, None, ALU.mult).then_inc(resets_ready, 1)
            v.tensor_scalar(member, low, float(NTP), None, ALU.mult)
            v.tensor_copy(target, high)
            done(v.engine_nop())
            done(v.tensor_tensor(table_row, member, target, ALU.add))
            v.tensor_scalar(row3(member), R[:, :, DST, :], 0.0, None, ALU.is_ge)
            v.tensor_scalar(row3(target), R[:, :, DST, :], float(P), None, ALU.is_lt)
            done(v.engine_nop())
            done(v.tensor_tensor(member, member, target, ALU.mult))
            done(v.tensor_tensor(row3(target), row3(table_row), by_row(dummy_row), ALU.subtract))
            done(v.tensor_tensor(target, target, member, ALU.mult))
            done(v.tensor_tensor(row3(target), row3(target), by_row(dummy_row), ALU.add))
            v.engine_nop().then_inc(field_ready, 1)
            n = 0
            for _, to in cols:
                for a, m in parts:
                    n += 1
                    dve.wait_ge(turned, n)
                    v.tensor_copy(to[:, a * P:(a + m) * P], s.bank(n % 2)[:, 0:m * P]).then_inc(columns, 1)

        @block.tensor
        def _(pe):
            pe.wait_ge(field_ready, 1)
            n = 0
            for of, _ in cols:
                for a, m in parts:
                    n += 1
                    if n > 2:
                        pe.wait_ge(columns, n - 2)
                    for c in range(m):
                        t = pe.transpose(s.bank(n % 2)[:, c * P:(c + 1) * P], of[:, a + c, :], s.ident[:, :])
                    t.then_inc(turned, 1)

        @block.sync
        def _(sp):
            sp.wait_ge(resets_ready, 1)
            sp.dma_start(s.reset_rows.rearrange("(c p e) -> p c e", p=P, e=P), row3(reset)).then_inc(rows_out, 16)
            attr_rows = s.attr_rows.rearrange("(c p f) e -> p c f e", p=P, f=4)
            for f in range(3):
                sp.dma_start(attr_rows[:, :, f, :], rows_v[:, :, EA + f, :]).then_inc(rows_out, 16)
            sp.dma_start(attr_rows[:, :, 3, :],
                         ones_edges.unsqueeze(1).broadcast_to((P, CH, P))).then_inc(rows_out, 16)
            sp.wait_ge(rows_out, 16 * 5)


def gather_rows(pool, s, table, ring_rows, slots, landed, rows_ready, free, released):
    def tick(base, b):
        wait(pool, rows_ready, base + b + 1)
        wait(pool, free, base + b - 3)
        pool.sem_inc(released, 1)
        for i in range(B4):
            pool.indirect_dma_start(ring_rows(b % 4, i), None, table,
                                    bass.IndirectOffsetOnAxis(ap=slots[:, b, i:i + 1], axis=0)).then_inc(landed[b % 4], 16)
    rounds(pool, tick, 0)
    for k in range(4):
        pool.wait_ge(landed[k], 16 * B4 * (NB // 4))


def steps4(base, b, lag=0):
    return bass.ds((base + (b - lag)) * B4, B4)


def pass_gin(nc, s, A):
    wk = Carver(s.work, s.pass0_at)
    onehot = wk.f32(2 * B4 * P).rearrange("p (r t n) -> p r t n", r=2, t=B4)
    ring = wk.f32(4 * B4 * C1).rearrange("p (r t f) -> p r t f", r=4, t=B4)
    slots = wk.i32(ROUND * B4).rearrange("p (r t) -> p r t", r=ROUND)
    targets = wk.f32(ROUND * B4).rearrange("p (r t) -> p r t", r=ROUND)
    same = wk.f32(B4 * P).rearrange("p (t n) -> p t n", t=B4)
    before = wk.f32(P)
    repeats = wk.f32(STEPS)
    sums = s.arena[:, 0:NTP * C1]
    sums_v = sums.rearrange("p (j f) -> p j f", f=C1)
    landed = [s.sem(f"gin_landed{k}") for k in range(4)]
    rows_ready, onehot_ready, part_ready, added, released = (
        s.sem("gin_" + n) for n in ("rows_ready", "onehot_ready", "part_ready", "added", "released"))
    targets_turned, same_ready, masked, repeats_ready, saved, cleared = (
        s.sem("gin_" + n) for n in ("targets_turned", "same_ready", "masked", "repeats_ready", "saved", "cleared"))
    last_work, counted, targets_ready = s.sem("gin_last_work"), s.sem("gin_counted"), s.sem("gin_targets_ready")
    PART, TURN = 0, 2

    with nc.Block() as block:
        @block.gpsimd
        def _(pool):
            gather_rows(pool, s, A["x"], lambda r, i: ring[:, r, i, 0:C], slots, landed, rows_ready, part_ready, released)

        @block.sync
        def _(sp):
            for n, layer in enumerate(s.tables):
                for k, table in enumerate(layer):
                    sp.wait_ge(part_ready, (n * K + k + 1) * (NB // (2 * K + 2)))
                    sp.dma_start(table.rearrange("(p r) f -> p (r f)", p=P).rearrange("p (n m) -> p n m", m=ZERO),
                                 s.zeros.unsqueeze(1).broadcast_to((P, NTP * F // ZERO, ZERO))).then_inc(cleared, 16)
            sp.wait_ge(cleared, 16 * 2 * K)
            sp.wait_ge(repeats_ready, 1)
            for n, t in enumerate((s.target_col, s.weight_col, s.scatter_row.bitcast(F32))):
                sp.dma_start(s.saved_cols[:, n * STEPS:(n + 1) * STEPS], t).then_inc(saved, 16)
            sp.wait_ge(saved, 16 * 3)

        @block.tensor
        def _(pe):
            def tick(base, b):
                if live(base, b, 1):
                    q = base + (b - 1)
                    pe.wait_ge(onehot_ready, q + 1)
                    pe.wait_ge(landed[(b - 1) % 4], landings(base, b - 1))
                    wait(pe, added, B4 * q - B4)
                    o = s.bank(PART + (b - 1) % 2)
                    for i in range(B4):
                        m = nc.tensor.matmul(o[:, i * C1:(i + 1) * C1], onehot[:, (b - 1) % 2, i, :],
                                             ring[:, (b - 1) % 4, i, :], start=True, stop=True)
                    m.then_inc(part_ready, 1)
                if live(base, b, 0):
                    pe.wait_ge(targets_ready, base + (b + 1))
                    wait(pe, same_ready, base + b)
                    for i in range(B4):
                        m = nc.tensor.transpose(s.bank(TURN)[:, i * P:(i + 1) * P],
                                                targets[:, b, i:i + 1].broadcast_to((P, P)), s.ident[:, :])
                    m.then_inc(targets_turned, 1)
            rounds(pe, tick, 1)

        @block.scalar
        def _(act):
            def tick(base, b):
                wait(act, same_ready, base + (b - 7))
                nc.scalar.copy(targets[:, b, :], s.target_col[:, steps4(base, b)]).then_inc(targets_ready, 1)
            rounds(act, tick, 0)

        @block.vector
        def _(dve):
            v = nc.vector
            v.memset(sums, 0.0).then_inc(added, B4)
            v.memset(ring[:, :, :, C:C1], 1.0)
            v.tensor_scalar(before, s.iota_row[:, :], s.iota_col[:, 0:1], None, ALU.is_lt)
            js = [dve.alloc_register(f"gin_tile{i}") for i in range(B4)]

            def tick(base, b):
                if live(base, b, 0):
                    wait(dve, part_ready, base + (b - 7))
                    v.tensor_copy(slots[:, b, :], s.feature_row[:, steps4(base, b)]).then_inc(rows_ready, 1)
                lag = 4
                if live(base, b, lag):
                    wait(dve, part_ready, base + (b - lag - 1))
                    v.tensor_tensor(onehot[:, b % 2], s.iota_row[:, :].unsqueeze(1).broadcast_to((P, B4, P)),
                                    s.rel_col[:, steps4(base, b, lag)].unsqueeze(2).broadcast_to((P, B4, P)),
                                    ALU.is_equal).then_inc(onehot_ready, 1)
                if live(base, b, lag + 1):
                    q = base + (b - lag - 1)
                    dve.load(js, s.node_tile[0:1, steps4(base, b, lag + 1)])
                    tiles = [dve.snap(dve.snap(j, min_val=0, max_val=NT - 1) * C1) for j in js]
                    dve.wait_ge(part_ready, q + 1)

                def add(i):
                    if live(base, b, lag + 1):
                        dve.wait_ge(added, q * B4 + (B4 + i))
                        to = sums[:, bass.ds(tiles[i], C1)]
                        part = s.bank(PART + (b - 1) % 2)[:, i * C1:(i + 1) * C1]
                        v.tensor_tensor(to, part, to, ALU.add).then_inc(added, 1)

                add(0)
                if live(base, b, lag):
                    q0 = base + (b - lag)
                    dve.wait_ge(targets_turned, q0 + 1)
                    wait(dve, counted, q0)
                    v.tensor_tensor(same, s.bank(TURN).rearrange("p (t n) -> p t n", t=B4),
                                    targets[:, (b - lag) % ROUND, :].unsqueeze(2).broadcast_to((P, B4, P)),
                                    ALU.is_equal).then_inc(same_ready, 1)
                add(1)
                if live(base, b, lag):
                    dve.wait_ge(same_ready, q0 + 1)
                    v.tensor_tensor(same, same, before.unsqueeze(1).broadcast_to((P, B4, P)), ALU.mult).then_inc(masked, 1)
                add(2)
                if live(base, b, lag):
                    dve.wait_ge(masked, q0 + 1)
                    v.tensor_reduce(repeats[:, steps4(base, b, lag)], same, AX_X, ALU.add).then_inc(counted, 1)
                add(3)

            rounds(dve, tick, 5)
            done = chain(dve, last_work)
            dve.wait_ge(counted, NB)
            dve.wait_ge(added, B4 * (NB + 1))
            target = same.rearrange("p t n -> p (t n)")
            for a in range(0, STEPS, B4 * P):
                m = min(B4 * P, STEPS - a)
                done(v.tensor_scalar(target[:, 0:m], s.target_col[:, a:a + m], s.dummy_col[:, 0:1], None, ALU.subtract))
                done(v.scalar_tensor_tensor(out=target[:, 0:m], in0=repeats[:, a:a + m], scalar=0.0, in1=target[:, 0:m],
                                            op0=ALU.is_equal, op1=ALU.mult))
                done(v.tensor_scalar(s.scatter_row[:, a:a + m], target[:, 0:m], s.dummy_col[:, 0:1], None, ALU.add))
            done(v.tensor_copy(s.count[:, :], sums_v[:, :, C]))
            v.engine_nop().then_inc(repeats_ready, 1)


def landings(base, b):
    return (base // 4 + (b // 4 + 1)) * (16 * B4) if isinstance(base, int) else base * (4 * B4) + (b // 4 + 1) * (16 * B4)


def layer_norm(nc, s, name, y, square, to):
    parts = 4
    m = NTP // parts
    wk = Carver(s.work, s.work.shape[1] - 3 * NTP)
    total, spread, scale = wk.f32(NTP), wk.f32(NTP), wk.f32(NTP)
    centred, squared, deviation, steps = (s.sem(f"{name}_{n}") for n in ("centred", "squared", "deviation", "norm_steps"))
    spread_ready = s.sem(name + "_spread_ready")
    over = lambda t: t.unsqueeze(2).broadcast_to((P, m, C))

    with nc.Block() as block:
        @block.vector
        def _(dve):
            v = nc.vector
            at = [slice(k * m, (k + 1) * m) for k in range(parts)]
            for k in range(parts):
                v.tensor_reduce(total[:, at[k]], y[:, at[k], :], AX_X, ALU.add).then_inc(steps, 1)
                dve.wait_ge(steps, 2 * k + 1)
                v.tensor_scalar(total[:, at[k]], total[:, at[k]], 1.0 / C, None, ALU.mult).then_inc(steps, 1)
                dve.wait_ge(steps, 2 * k + 2)
                v.tensor_tensor(y[:, at[k], :], y[:, at[k], :], over(total[:, at[k]]), ALU.subtract).then_inc(centred, 1)
            for k in range(parts):
                dve.wait_ge(squared, k + 1)
                v.tensor_reduce(spread[:, at[k]], square[:, at[k], :], AX_X, ALU.add).then_inc(spread_ready, 1)
            for k in range(parts):
                dve.wait_ge(deviation, k + 1)
                v.reciprocal(scale[:, at[k]], spread[:, at[k]]).then_inc(steps, 1)
                dve.wait_ge(steps, 2 * parts + k + 1)
                dve.wait_ge(centred, k + 1)
                v.tensor_tensor(to[:, at[k], :], y[:, at[k], :], over(scale[:, at[k]]), ALU.mult)

        @block.scalar
        def _(act):
            at = [slice(k * m, (k + 1) * m) for k in range(parts)]
            for k in range(parts):
                act.wait_ge(centred, k + 1)
                nc.scalar.activation(square[:, at[k], :], y[:, at[k], :], ACT.Square).then_inc(squared, 1)
            for k in range(parts):
                act.wait_ge(spread_ready, k + 1)
                nc.scalar.activation(spread[:, at[k]], spread[:, at[k]], ACT.Sqrt, bias=s.eps_col[:, 0:1],
                                     scale=1.0 / C).then_inc(deviation, 1)


def tiles_of(view, g):
    return view[:, bass.ds(g * GRP, GRP), :]


def turn_group(nc, s, of, to, rows):
    for t in range(GRP):
        ins = nc.tensor.transpose(to[0:rows, t * P:(t + 1) * P], of[:, t, 0:rows], s.ident[:, :])
    return ins


def node_gin(nc, s, A):
    sums = s.arena[:, 0:NTP * C1].rearrange("p (j f) -> p j f", f=C1)
    ar = Carver(s.arena, NTP * C1)
    y, square = (ar.f32(NTP * C).rearrange("p (j f) -> p j f", f=C) for _ in range(2))
    wk = Carver(s.work)
    W1, b1, W2, b2 = wk.f32(HID)[0:C, :], wk.f32(1), wk.f32(C), wk.f32(C)[0:1, :]
    hT, hidden = wk.f32(GRP * P), wk.f32(GRP * P)
    h = wk.f32(GRP * C1).rearrange("p (t f) -> p t f", t=GRP)
    loaded, h_ready, hT_psum, hT_ready, hidden_psum, hidden_ready, out_psum, y_ready = (
        s.sem("gin_node_" + n) for n in ("loaded", "h_ready", "hT_psum", "hT_ready", "hidden_psum", "hidden_ready",
                                         "out_psum", "y_ready"))
    TURN, HIDDEN, OUT = 0, 1, 2

    with nc.Block() as block:
        @block.sync
        def _(sp):
            sp.dma_start(W1, A["L0_gnn_W1"]).then_inc(loaded, 16)
            sp.dma_start(W2, A["L0_gnn_W2"]).then_inc(loaded, 16)
            sp.dma_start(b2, A["L0_gnn_b2"].unsqueeze(0)).then_inc(loaded, 16)
            with nc.allow_non_contiguous_dma(reason="a bias by partition"):
                sp.dma_start(b1, A["L0_gnn_b1"].unsqueeze(1)).then_inc(loaded, 16)
            sp.wait_ge(loaded, 64)

        @block.vector
        def _(dve):
            v = nc.vector

            def tick(g):
                if group_live(g, 0):
                    wait(dve, hT_psum, g)
                    v.scalar_tensor_tensor(out=h, in0=tiles_of(s.Xv, g), scalar=s.one_eps[:, 0:1],
                                           in1=tiles_of(sums, g), op0=ALU.mult, op1=ALU.add).then_inc(h_ready, 1)
                if group_live(g, 2):
                    dve.wait_ge(out_psum, g - 1)
                    v.tensor_tensor(tiles_of(y, g - 2), s.bank(OUT)[:, 0:GRP * C].rearrange("p (t f) -> p t f", t=GRP),
                                    tiles_of(s.Xv, g - 2)[:, :, 0:C], ALU.add).then_inc(y_ready, 1)
            pipeline(dve, tick, 2)

        @block.scalar
        def _(act):
            act.wait_ge(loaded, 64)

            def tick(g):
                if group_live(g, 1):
                    act.wait_ge(hidden_psum, g)
                    nc.scalar.activation(hidden, s.bank(HIDDEN), ACT.Relu, bias=b1[:, 0:1]).then_inc(hidden_ready, 1)
                if group_live(g, 0):
                    act.wait_ge(hT_psum, g + 1)
                    wait(act, hidden_psum, g)
                    nc.scalar.copy(hT[0:C, :], s.bank(TURN)[0:C, :]).then_inc(hT_ready, 1)
            pipeline(act, tick, 2)

        @block.tensor
        def _(pe):
            pe.wait_ge(loaded, 64)

            def tick(g):
                if group_live(g, 0):
                    pe.wait_ge(h_ready, g + 1)
                    wait(pe, hT_ready, g)
                    turn_group(nc, s, h, s.bank(TURN), C1).then_inc(hT_psum, 1)
                if group_live(g, 2):
                    pe.wait_ge(hidden_ready, g - 1)
                    wait(pe, y_ready, g - 2)
                    for t in range(GRP):
                        to = s.bank(OUT)[:, t * C:(t + 1) * C]
                        nc.tensor.matmul(to, s.ones_row[:, :], b2, start=True, stop=False)
                        m = nc.tensor.matmul(to, hidden[:, t * P:(t + 1) * P], W2, start=False, stop=True)
                    m.then_inc(out_psum, 1)
                if group_live(g, 1):
                    pe.wait_ge(hT_ready, g)
                    wait(pe, hidden_ready, g - 1)
                    nc.tensor.matmul(s.bank(HIDDEN), W1, hT[0:C, :], start=True, stop=True).then_inc(hidden_psum, 1)
            pipeline(pe, tick, 2)
    layer_norm(nc, s, "gin_norm", y, square, s.Xv[:, :, 0:C])


def messages_pna(nc, s, A):
    wk = Carver(s.work)
    stack, Wpre = wk.f32(C), wk.f32(3 * C)[0:C, :].rearrange("p (k f) -> p k f", k=3)
    stackT, both = wk.f32(C + 4)[0:C, :], wk.f32(2 * C)[0:C, :]
    x = wk.f32(GRP * C1).rearrange("p (t f) -> p t f", t=GRP)
    xT = wk.f32(GRP * P)
    attr_weight = wk.f32(C)[0:4, :]
    by_src = s.arena[:, 0:NTP * C].rearrange("p (j f) -> p j f", f=C)
    loaded, stack_turned, stack_ready, products, weights_ready, kept, stored = (
        s.sem("msg_" + n) for n in ("loaded", "stack_turned", "stack_ready", "products", "weights_ready", "kept", "stored"))
    x_ready, xT_psum, xT_ready, out_psum, dst_ready, src_ready = (
        s.sem("msg_" + n) for n in ("x_ready", "xT_psum", "xT_ready", "out_psum", "dst_ready", "src_ready"))
    placed = s.sem("msg_placed")
    TURN, OUT, SMALL = 0, 1, 2
    R = C + 4

    with nc.Block() as block:
        @block.sync
        def _(sp):
            sp.dma_start(stack[0:C, :], A["L1_gnn_W"]).then_inc(loaded, 16)
            sp.dma_start(stack[C:C + 3, :], A["L1_gnn_We"]).then_inc(loaded, 16)
            sp.dma_start(stack[C + 3:R, :], A["L1_gnn_be"].unsqueeze(0)).then_inc(loaded, 16)
            sp.dma_start(Wpre, A["L1_gnn_Wpre"].rearrange("(k p) f -> p k f", p=C)).then_inc(loaded, 16)
            sp.dma_start(s.x_saved, s.X[:, :]).then_inc(kept, 16)
            sp.wait_ge(weights_ready, 2)
            for i in range(B4):
                sp.dma_start(s.attr_weight[i * 4:(i + 1) * 4, i * C:(i + 1) * C], attr_weight).then_inc(placed, 16)
            sp.wait_ge(placed, 16 * B4)
            sp.wait_ge(src_ready, GROUPS)
            sp.dma_start(s.message_table.rearrange("(p r) f -> p (r f)", p=P), s.arena[:, 0:NTP * C]).then_inc(stored, 16)
            sp.wait_ge(stored, 16)

        @block.tensor
        def _(pe):
            pe.wait_ge(loaded, 64)
            nc.tensor.transpose(s.bank(SMALL)[0:C, 0:R], stack[0:R, :], s.ident[0:R, 0:R]).then_inc(stack_turned, 1)
            pe.wait_ge(stack_ready, 1)
            nc.tensor.matmul(s.bank(SMALL)[0:C, 0:C], stackT[:, 0:C], Wpre[:, 1, :], start=True, stop=True)
            nc.tensor.matmul(s.bank(SMALL)[0:C, C:2 * C], stackT[:, 0:C], Wpre[:, 0, :], start=True, stop=True)
            nc.tensor.matmul(s.bank(SMALL)[0:4, 2 * C:3 * C], stackT[:, C:R], Wpre[:, 2, :], start=True, stop=True).then_inc(products, 1)
            pe.wait_ge(weights_ready, 2)

            def tick(g):
                if group_live(g, 0):
                    pe.wait_ge(x_ready, g + 1)
                    wait(pe, xT_ready, g)
                    turn_group(nc, s, x, s.bank(TURN), C1).then_inc(xT_psum, 1)
                if group_live(g, 1):
                    pe.wait_ge(xT_ready, g)
                    wait(pe, dst_ready, g - 1)
                    wait(pe, src_ready, g - 1)
                    for t in range(GRP):
                        m = nc.tensor.matmul(s.bank(OUT)[:, t * 2 * C:(t + 1) * 2 * C], xT[0:C, t * P:(t + 1) * P], both,
                                             start=True, stop=True)
                    m.then_inc(out_psum, 1)
            pipeline(pe, tick, 1)

        @block.vector
        def _(dve):
            v = nc.vector
            dve.wait_ge(stack_turned, 1)
            v.tensor_copy(stackT, s.bank(SMALL)[0:C, 0:R]).then_inc(stack_ready, 1)
            dve.wait_ge(products, 1)
            v.tensor_copy(both, s.bank(SMALL)[0:C, 0:2 * C]).then_inc(weights_ready, 1)
            v.memset(s.attr_weight[:, :], 0.0)
            v.tensor_copy(attr_weight, s.bank(SMALL)[0:4, 2 * C:3 * C]).then_inc(weights_ready, 1)
            dve.wait_ge(kept, 16)

            def tick(g):
                if group_live(g, 0):
                    wait(dve, xT_psum, g)
                    v.tensor_copy(x, tiles_of(s.Xv, g)).then_inc(x_ready, 1)
                if group_live(g, 1):
                    dve.wait_ge(out_psum, g)
                    wait(dve, src_ready, g)
                    v.tensor_copy(tiles_of(s.Xv, g - 1)[:, :, 0:C],
                                  s.bank(OUT).rearrange("p (t f) -> p t f", t=GRP)[:, :, C:2 * C]).then_inc(dst_ready, 1)
            pipeline(dve, tick, 1)

        @block.scalar
        def _(act):
            def tick(g):
                if group_live(g, 1):
                    act.wait_ge(out_psum, g)
                    nc.scalar.copy(tiles_of(by_src, g - 1),
                                   s.bank(OUT).rearrange("p (t f) -> p t f", t=GRP)[:, :, 0:C]).then_inc(src_ready, 1)
                if group_live(g, 0):
                    act.wait_ge(xT_psum, g + 1)
                    wait(act, out_psum, g)
                    nc.scalar.copy(xT[0:C, :], s.bank(TURN)[0:C, :]).then_inc(xT_ready, 1)
            pipeline(act, tick, 1)


def pass_pna(nc, s, A):
    wk = Carver(s.work)
    onehot = wk.f32(4 * B4 * P).rearrange("p (r t n) -> p r t n", r=4, t=B4)
    parts = wk.f32(4 * B4 * 5 * C).rearrange("p (r t f) -> p r t f", r=4, t=B4)
    spread = wk.f32(2 * B4 * P).rearrange("p (r t n) -> p r t n", r=2, t=B4)
    running = wk.f32(2 * B4 * P).rearrange("p (r n) -> p r n", r=2)
    resets = wk.bf16(4 * B4 * P).rearrange("p (r n) -> p r n", r=4)
    attrs = wk.f32(2 * P).rearrange("p (r n) -> p r n", r=2)[0:B4 * 4]
    ring = wk.f32(4 * B4 * C).rearrange("p (r t f) -> p r t f", r=4, t=B4)
    u_sum = wk.f32(B4 * C).rearrange("p (t f) -> p t f", t=B4)
    slots = wk.i32(ROUND * B4).rearrange("p (r t) -> p r t", r=ROUND)
    sums = s.arena[:, :]
    W4 = 4 * C
    names = ("rows_ready", "onehot_ready", "onehot_turned", "spread_ready", "u_psum", "u_summed", "u_ready",
             "negated", "squared", "u_turned", "maxima_ready", "maxima_turned", "maxima_back", "part_ready",
             "added", "released")
    (rows_ready, onehot_ready, onehot_turned, spread_ready, u_psum, u_summed, u_ready, negated, squared, u_turned,
     maxima_ready, maxima_turned, maxima_back, part_ready, added, released) = (s.sem("pna_" + n) for n in names)
    released_loads = s.sem("pna_released_loads")
    landed = [s.sem(f"pna_landed{k}") for k in range(4)]
    resets_landed = [s.sem(f"pna_resets_landed{k}") for k in range(4)]
    attrs_landed = [s.sem(f"pna_attrs_landed{k}") for k in range(2)]
    SPREAD, MESSAGE, TURN, BACK, PART = 0, 1, 2, 3, 4

    def loads(base, b, r):
        return base * (16 // r) + (b // r + 1) * 16

    with nc.Block() as block:
        @block.gpsimd
        def _(pool):
            gather_rows(pool, s, s.message_table, lambda r, i: ring[:, r, i, :], slots, landed, rows_ready, u_summed, released)

        @block.sync
        def _(sp):
            def tick(base, b):
                q = base + b
                wait(sp, u_psum, q - 1)
                sp.dma_start(attrs[:, b % 2, :], s.attr_rows[bass.ds(q * (B4 * 4), B4 * 4), :]).then_inc(attrs_landed[b % 2], 16)
                wait(sp, maxima_ready, q - 3)
                sp.sem_inc(released_loads, 1)
                sp.dma_start(resets[:, b % 4, :], s.reset_rows[bass.ds(q * (B4 * P), B4 * P)].partition_broadcast(P))\
                    .then_inc(resets_landed[b % 4], 16)
            rounds(sp, tick, 0)
            for k in range(2):
                sp.wait_ge(attrs_landed[k], 8 * NB)
            for k in range(4):
                sp.wait_ge(resets_landed[k], 4 * NB)

        @block.tensor
        def _(pe):
            js = [pe.alloc_register(f"pna_pe_tile{i}") for i in range(B4)]

            def tick(base, b):
                if live(base, b, 1):
                    pe.load(js, s.node_tile[0:1, steps4(base, b, 1)])
                    tiles = [pe.snap(pe.snap(j, min_val=0, max_val=NT - 1) * C1) for j in js]
                if live(base, b, 4):
                    q = base + (b - 4)
                    pe.wait_ge(maxima_back, q + 1)
                    pe.wait_ge(squared, q + 1)
                    wait(pe, added, B4 * q)
                    for i in range(B4):
                        m = nc.tensor.matmul(s.bank(PART + b % 2 * 2, 2)[:, i * W4:(i + 1) * W4], onehot[:, (b - 4) % 4, i, :],
                                             parts[:, (b - 4) % 4, i, C:5 * C], start=True, stop=True)
                    m.then_inc(part_ready, 1)
                if live(base, b, 3):
                    q = base + (b - 3)
                    pe.wait_ge(maxima_ready, q + 1)
                    wait(pe, maxima_back, q)
                    for i in range(B4):
                        m = nc.tensor.transpose(s.bank(BACK)[:, i * P:(i + 1) * P], running[:, (b - 3) % 2, i * P:(i + 1) * P], s.ident[:, :])
                    m.then_inc(maxima_turned, 1)
                if live(base, b, 1):
                    q = base + (b - 1)
                    pe.wait_ge(attrs_landed[(b - 1) % 2], loads(base, b - 1, 2))
                    pe.wait_ge(spread_ready, q + 1)
                    wait(pe, u_summed, q)
                    nc.tensor.matmul(s.bank(MESSAGE)[:, 0:B4 * C], attrs[:, (b - 1) % 2, :], s.attr_weight[:, :], start=True, stop=False)
                    for i in range(B4):
                        m = nc.tensor.matmul(s.bank(MESSAGE)[:, i * C:(i + 1) * C], spread[:, (b - 1) % 2, i, :],
                                             s.X[:, bass.ds(tiles[i], C)], start=False, stop=i == B4 - 1)
                    m.then_inc(u_psum, 1)
                if live(base, b, 2):
                    q = base + (b - 2)
                    pe.wait_ge(negated, q + 1)
                    wait(pe, maxima_ready, q)
                    for i in range(B4):
                        m = nc.tensor.transpose(s.bank(TURN)[:, i * P:(i + 1) * P], parts[:, (b - 2) % 4, i, 0:2 * C], s.ident[:, :])
                    m.then_inc(u_turned, 1)
                if live(base, b, 0):
                    q = base + b
                    pe.wait_ge(onehot_ready, q + 1)
                    wait(pe, spread_ready, q)
                    for i in range(B4):
                        m = nc.tensor.transpose(s.bank(SPREAD)[:, i * P:(i + 1) * P], onehot[:, b % 4, i, :], s.ident[:, :])
                    m.then_inc(onehot_turned, 1)
            rounds(pe, tick, 4)

        @block.scalar
        def _(act):
            def tick(base, b):
                if live(base, b, 3):
                    q = base + (b - 3)
                    act.wait_ge(maxima_turned, q + 1)
                    for i in range(B4):
                        m = nc.scalar.activation(parts[:, (b - 3) % 4, i, 3 * C:5 * C], s.bank(BACK)[:, i * P:(i + 1) * P], ACT.Copy,
                                                 scale=s.last_col[:, bass.ds(q * B4 + i, 1)])
                    m.then_inc(maxima_back, 1)
                u = parts[:, (b - 1) % 4, :, C:2 * C]
                if live(base, b, 1):
                    act.wait_ge(u_ready, base + b)
                    nc.scalar.mul(parts[:, (b - 1) % 4, :, 0:C], u, -1.0).then_inc(negated, 1)
                if live(base, b, 0):
                    act.wait_ge(onehot_turned, base + (b + 1))
                    wait(act, u_psum, base + (b - 1))
                    nc.scalar.copy(spread[:, b % 2], s.bank(SPREAD).rearrange("p (t n) -> p t n", t=B4)).then_inc(spread_ready, 1)
                if live(base, b, 1):
                    nc.scalar.square(parts[:, (b - 1) % 4, :, 2 * C:3 * C], u).then_inc(squared, 1)
            rounds(act, tick, 3)

        @block.vector
        def _(dve):
            v = nc.vector
            for k in range(B4):
                v.memset(sums[:, k * (NTP * C):(k + 1) * (NTP * C)], 0.0).then_inc(added, 1)
            v.memset(running[:, 1, :], NEG)
            js = [dve.alloc_register(f"pna_tile{i}") for i in range(B4)]
            LAG = 4

            def tick(base, b):
                if live(base, b, 0):
                    wait(dve, u_psum, base + (b - 7))
                    v.tensor_copy(slots[:, b, :], s.message_row[:, steps4(base, b)]).then_inc(rows_ready, 1)
                if live(base, b, LAG):
                    wait(dve, part_ready, base + (b - LAG - 3))
                    v.tensor_tensor(onehot[:, b % 4], s.iota_row[:, :].unsqueeze(1).broadcast_to((P, B4, P)),
                                    s.rel_col[:, steps4(base, b, LAG)].unsqueeze(2).broadcast_to((P, B4, P)),
                                    ALU.is_equal).then_inc(onehot_ready, 1)
                lag = LAG + 4
                if live(base, b, lag):
                    qa = base + (b - lag)
                    dve.load(js, s.node_tile[0:1, steps4(base, b, lag)])
                    tiles = [dve.snap(dve.snap(j, min_val=0, max_val=NT - 1) * W4) for j in js]
                    dve.wait_ge(part_ready, qa + 1)

                def add(i):
                    if live(base, b, LAG + 4):
                        dve.wait_ge(added, qa * B4 + (B4 + i))
                        to = sums[:, bass.ds(tiles[i], W4)]
                        v.tensor_tensor(to, s.bank(PART + b % 2 * 2, 2)[:, i * W4:(i + 1) * W4], to, ALU.add).then_inc(added, 1)

                add(0)
                if live(base, b, LAG + 1):
                    r = b - LAG - 1
                    q = base + r
                    dve.wait_ge(landed[r % 4], landings(base, r))
                    dve.wait_ge(u_psum, q + 1)
                    wait(dve, u_ready, q)
                    v.tensor_tensor(u_sum, s.bank(MESSAGE)[:, 0:B4 * C].rearrange("p (t f) -> p t f", t=B4), ring[:, r % 4],
                                    ALU.add).then_inc(u_summed, 1)
                add(1)
                if live(base, b, LAG + 1):
                    dve.wait_ge(u_summed, q + 1)
                    v.tensor_tensor(parts[:, r % 4, :, C:2 * C], u_sum,
                                    s.ew_col[:, steps4(base, b, LAG + 1)].unsqueeze(2).broadcast_to((P, B4, C)),
                                    ALU.mult).then_inc(u_ready, 1)
                add(2)
                if live(base, b, LAG + 2):
                    r2 = b - LAG - 2
                    q2 = base + r2
                    dve.wait_ge(u_turned, q2 + 1)
                    dve.wait_ge(resets_landed[r2 % 4], loads(base, r2, 4))
                    wait(dve, maxima_turned, q2 - 1)
                    wait(dve, maxima_ready, q2)
                    v.tensor_tensor_scan(running[:, r2 % 2, :], resets[:, r2 % 4, :], s.bank(TURN),
                                         running[:, (r2 + 1) % 2, B4 * P - 1:B4 * P], ALU.add, ALU.max).then_inc(maxima_ready, 1)
                add(3)
            rounds(dve, tick, LAG + 4)


def node_pna_out(nc, s, A):
    sums = s.arena[:, :].rearrange("p (j f) -> p j f", f=4 * C)
    wk = Carver(s.work)
    Wagg = wk.f32(2 * 3 * C).rearrange("p (k f) -> p k f", k=2)
    W, Wm, Wx = wk.f32(C)[0:C, :], wk.f32(C)[0:C, :], wk.f32(C)[0:C1, :]
    WT, bpre = wk.f32(C)[0:C, :], wk.f32(C)
    scale_n, has, deg, logd, s2, s3 = (wk.f32(NTP) for _ in range(6))
    vec, logs, log_sum, avg, avg_inv = wk.f32(NTP), wk.f32(NTP), wk.f32(1), wk.f32(1), wk.f32(1)
    ones_col = wk.f32(P)
    agg = wk.f32(2 * GRP * 4 * C).rearrange("p (r t f) -> p r t f", r=2, t=GRP)
    squares, shift = (wk.f32(GRP * C).rearrange("p (t f) -> p t f", t=GRP) for _ in range(2))
    x = wk.f32(GRP * C1).rearrange("p (t f) -> p t f", t=GRP)
    aggT0, aggT1, xT = wk.f32(GRP * P), wk.f32(GRP * P), wk.f32(GRP * P)
    o1, o2 = (wk.f32(GRP * C).rearrange("p (t f) -> p t f", t=GRP) for _ in range(2))
    names = ("loaded", "x_loaded", "scalars", "logs_ready", "mean_log", "W_turned", "W_ready", "Wx_psum", "Wx_ready",
             "work", "agg_ready", "x_ready", "deviation", "turned", "agg_turned", "out_psum", "out_ready", "combine",
             "variance")
    (loaded, x_loaded, scalars, logs_ready, mean_log, W_turned, W_ready, Wx_psum, Wx_ready,
     work, agg_ready, x_ready, deviation, turned, agg_turned, out_psum, out_ready, combine,
     variance) = (s.sem("pna_out_" + n) for n in names)
    TURN, OUT, SMALL = 0, 3, 5
    NV = N // NTP
    over = lambda t: t.unsqueeze(2).broadcast_to((P, GRP, C))
    group_col = lambda t, g: t[:, bass.ds(g * GRP, GRP)]
    cols = lambda t: t.rearrange("p (t f) -> p t f", t=GRP)
    n_loaded = 9 + 6

    with nc.Block() as block:
        @block.sync
        def _(sp):
            sp.dma_start(s.X[:, :], s.x_saved).then_inc(x_loaded, 16)
            for k in range(3):
                at = C + 4 * C * k
                to = slice(k * C, (k + 1) * C)
                sp.dma_start(Wagg[0:C, 0, to], A["L1_gnn_Wpost"][at:at + C, :]).then_inc(loaded, 16)
                sp.dma_start(Wagg[C:P, 0, to], A["L1_gnn_Wpost"][at + 3 * C:at + 4 * C, :]).then_inc(loaded, 16)
                sp.dma_start(Wagg[:, 1, to], A["L1_gnn_Wpost"][at + C:at + 3 * C, :]).then_inc(loaded, 16)
            sp.dma_start(W, A["L1_gnn_W"]).then_inc(loaded, 16)
            sp.dma_start(Wm, A["L1_gnn_Wpost"][0:C, :]).then_inc(loaded, 16)
            sp.dma_start(Wx[C:C1, :], A["L1_gnn_bpost"].unsqueeze(0)).then_inc(loaded, 16)
            sp.dma_start(bpre, A["L1_gnn_bpre"].partition_broadcast(P)).then_inc(loaded, 16)
            sp.dma_start(vec[0:NV, :], A["node_vec"].rearrange("(p j) -> p j", p=NV)).then_inc(loaded, 16)
            sp.dma_start(vec[NV:P, :], A["node_vec"][0:(P - NV) * NTP].rearrange("(p j) -> p j", p=P - NV)).then_inc(loaded, 16)
            sp.wait_ge(loaded, 16 * n_loaded)

        @block.vector
        def _(dve):
            v = nc.vector
            done = chain(dve, scalars)
            v.memset(ones_col, 1.0)
            v.tensor_scalar(has, s.count[:, :], 1.0, None, ALU.min)
            done(v.tensor_scalar(deg, s.count[:, :], 1.0, None, ALU.max))
            done(v.reciprocal(scale_n, deg))
            dve.wait_ge(loaded, 16 * n_loaded)
            dve.wait_ge(x_loaded, 16)
            dve.wait_ge(W_turned, 1)
            v.tensor_copy(WT, s.bank(SMALL)[0:C, 0:C]).then_inc(W_ready, 1)
            dve.wait_ge(Wx_psum, 1)
            v.tensor_copy(Wx[0:C, :], s.bank(SMALL)[0:C, 0:C]).then_inc(Wx_ready, 1)
            dve.wait_ge(mean_log, 1)
            done(v.tensor_scalar(avg, s.bank(SMALL)[:, C:C + 1], 1.0 / N, None, ALU.mult))
            done(v.reciprocal(avg_inv, avg))
            done(v.reciprocal(s3, logd))
            v.tensor_scalar(s2, logd, avg_inv[:, 0:1], None, ALU.mult)
            done(v.tensor_scalar(s3, s3, avg[:, 0:1], None, ALU.mult))
            done(v.tensor_tensor(s3, s3, s2, ALU.mult))

            def tick(g):
                if group_live(g, 0):
                    a = agg[:, 0]
                    wait(dve, turned, g)
                    v.tensor_tensor(a[:, :, 0:2 * C], tiles_of(sums, g)[:, :, 0:2 * C],
                                    group_col(scale_n, g).unsqueeze(2).broadcast_to((P, GRP, 2 * C)), ALU.mult).then_inc(work, 1)
                    v.tensor_copy(x, tiles_of(s.Xv, g)).then_inc(x_ready, 1)
                    v.tensor_tensor(shift, over(group_col(has, g)), bpre.unsqueeze(1).broadcast_to((P, GRP, C)), ALU.mult).then_inc(work, 1)
                    dve.wait_ge(work, g * 4 + 1)
                    v.tensor_tensor(squares, a[:, :, 0:C], a[:, :, 0:C], ALU.mult).then_inc(work, 1)
                    dve.wait_ge(work, g * 4 + 3)
                    v.tensor_tensor(a[:, :, C:2 * C], a[:, :, C:2 * C], squares, ALU.subtract).then_inc(variance, 1)
                    v.tensor_tensor(a[:, :, 0:C], a[:, :, 0:C], shift, ALU.add)
                    v.tensor_tensor(a[:, :, 2 * C:3 * C], shift, tiles_of(sums, g)[:, :, 2 * C:3 * C], ALU.subtract)
                    v.tensor_tensor(a[:, :, 3 * C:4 * C], shift, tiles_of(sums, g)[:, :, 3 * C:4 * C], ALU.add).then_inc(agg_ready, 1)
                    v.engine_nop().then_inc(work, 1)
                if group_live(g, 1):
                    dve.wait_ge(out_psum, g)
                    out4 = s.bank(OUT, 2).rearrange("p (t f) -> p t f", t=GRP)
                    v.tensor_tensor(o1, out4[:, :, C:2 * C], over(group_col(s2, g - 1)), ALU.mult)
                    v.tensor_tensor(o2, out4[:, :, 2 * C:3 * C], over(group_col(s3, g - 1)), ALU.mult).then_inc(combine, 1)
                    dve.wait_ge(combine, (g - 1) * 2 + 1)
                    v.tensor_tensor(o1, o1, o2, ALU.add).then_inc(combine, 1)
                    dve.wait_ge(combine, (g - 1) * 2 + 2)
                    v.tensor_tensor(tiles_of(sums, g - 1)[:, :, 0:C], out4[:, :, 0:C], o1, ALU.add).then_inc(out_ready, 1)
            pipeline(dve, tick, 1)

        @block.scalar
        def _(act):
            act.wait_ge(loaded, 16 * n_loaded)
            nc.scalar.activation(logs[0:NV, :], vec[0:NV, :], ACT.Ln, bias=1.0, accum_out=log_sum[0:NV, :]).then_inc(logs_ready, 1)
            act.wait_ge(scalars, 1)
            nc.scalar.activation(logd, deg, ACT.Ln, bias=1.0).then_inc(logs_ready, 1)

            def tick(g):
                if group_live(g, 0):
                    std = agg[:, 0, :, C:2 * C]
                    act.wait_ge(variance, g + 1)
                    nc.scalar.activation(std, std, ACT.Relu).then_inc(deviation, 1)
                    act.wait_ge(deviation, g * 2 + 1)
                    nc.scalar.activation(std, std, ACT.Sqrt, bias=s.eps_col[:, 0:1]).then_inc(deviation, 1)
                    act.wait_ge(turned, g + 1)
                    wait(act, out_psum, g)
                    nc.scalar.copy(xT[0:C1, :], s.bank(TURN + 2)[0:C1, :])
                    nc.scalar.copy(aggT0, s.bank(TURN))
                    nc.scalar.copy(aggT1, s.bank(TURN + 1)).then_inc(agg_turned, 1)
            pipeline(act, tick, 0)

        @block.tensor
        def _(pe):
            t_ = nc.tensor
            pe.wait_ge(loaded, 16 * n_loaded)
            t_.transpose(s.bank(SMALL)[0:C, 0:C], W, s.ident[0:C, 0:C]).then_inc(W_turned, 1)
            pe.wait_ge(W_ready, 1)
            t_.matmul(s.bank(SMALL)[0:C, 0:C], WT, Wm, start=True, stop=True).then_inc(Wx_psum, 1)
            pe.wait_ge(Wx_ready, 1)
            pe.wait_ge(logs_ready, 2)
            t_.matmul(s.bank(SMALL)[:, C:C + 1], ones_col[0:NV, :], log_sum[0:NV, :], start=True, stop=True).then_inc(mean_log, 1)

            def tick(g):
                if group_live(g, 0):
                    pe.wait_ge(agg_ready, g + 1)
                    pe.wait_ge(x_ready, g + 1)
                    pe.wait_ge(deviation, g * 2 + 2)
                    wait(pe, agg_turned, g)
                    turn_group(nc, s, agg[:, 0, :, 0:P], s.bank(TURN), P)
                    turn_group(nc, s, agg[:, 0, :, P:2 * P], s.bank(TURN + 1), P)
                    turn_group(nc, s, x, s.bank(TURN + 2), C1).then_inc(turned, 1)
                if group_live(g, 1):
                    pe.wait_ge(agg_turned, g)
                    wait(pe, out_ready, g - 1)
                    for t in range(GRP):
                        to, at = s.bank(OUT, 2)[:, t * 4 * C:t * 4 * C + 3 * C], slice(t * P, (t + 1) * P)
                        t_.matmul(to, aggT0[:, at], Wagg[:, 0, :], start=True, stop=False)
                        t_.matmul(to, aggT1[:, at], Wagg[:, 1, :], start=False, stop=False)
                        m = t_.matmul(to[:, 0:C], xT[0:C1, at], Wx, start=False, stop=True)
                    m.then_inc(out_psum, 1)
            pipeline(pe, tick, 1)


def node_pna_gru(nc, s, A):
    sums = s.arena[:, :].rearrange("p (j f) -> p j f", f=4 * C)
    y, square = sums[:, :, C:2 * C], sums[:, :, 2 * C:3 * C]
    wk = Carver(s.work)
    Wih, Whh = wk.f32(3 * C)[0:C1, :], wk.f32(3 * C)[0:C1, :]
    o = wk.f32(GRP * C1).rearrange("p (t f) -> p t f", t=GRP)
    x = wk.f32(GRP * C1).rearrange("p (t f) -> p t f", t=GRP)
    oT, xT = wk.f32(GRP * P), wk.f32(GRP * P)
    rz = wk.f32(GRP * 2 * C).rearrange("p (t f) -> p t f", t=GRP)
    new, diff = (wk.f32(GRP * C).rearrange("p (t f) -> p t f", t=GRP) for _ in range(2))
    names = ("loaded", "ones", "inputs_ready", "turned", "turned_back", "gates_psum", "gates_ready", "new_steps",
             "new_sum", "new_ready", "y_ready", "mix")
    (loaded, ones, inputs_ready, turned, turned_back, gates_psum, gates_ready, new_steps,
     new_sum, new_ready, y_ready, mix) = (s.sem("gru_" + n) for n in names)
    TURN, GATES = 0, 2
    gates = s.bank(GATES, 2).rearrange("p (t f) -> p t f", t=GRP)

    with nc.Block() as block:
        @block.sync
        def _(sp):
            sp.dma_start(Wih[0:C, :], A["L1_gnn_Wih"]).then_inc(loaded, 16)
            sp.dma_start(Wih[C:C1, :], A["L1_gnn_bih"].unsqueeze(0)).then_inc(loaded, 16)
            sp.dma_start(Whh[0:C, :], A["L1_gnn_Whh"]).then_inc(loaded, 16)
            sp.dma_start(Whh[C:C1, :], A["L1_gnn_bhh"].unsqueeze(0)).then_inc(loaded, 16)
            sp.wait_ge(loaded, 64)

        @block.vector
        def _(dve):
            v = nc.vector
            v.memset(o[:, :, C:C1], 1.0).then_inc(ones, 1)

            def tick(g):
                if group_live(g, 0):
                    wait(dve, turned, g)
                    v.tensor_copy(o[:, :, 0:C], tiles_of(sums, g)[:, :, 0:C])
                    v.tensor_copy(x, tiles_of(s.Xv, g)).then_inc(inputs_ready, 1)
                if group_live(g, 1):
                    q = g - 1
                    dve.wait_ge(gates_ready, g)
                    v.tensor_tensor(new, rz[:, :, 0:C], gates[:, :, 3 * C:4 * C], ALU.mult).then_inc(new_steps, 1)
                    dve.wait_ge(new_steps, q + 1)
                    v.tensor_tensor(new, new, gates[:, :, 2 * C:3 * C], ALU.add).then_inc(new_sum, 1)
                    dve.wait_ge(new_ready, q + 1)
                    xs = tiles_of(s.Xv, q)[:, :, 0:C]
                    v.tensor_tensor(diff, xs, new, ALU.subtract).then_inc(mix, 1)
                    dve.wait_ge(mix, q * 3 + 1)
                    v.tensor_tensor(diff, diff, rz[:, :, C:2 * C], ALU.mult).then_inc(mix, 1)
                    v.tensor_tensor(new, new, xs, ALU.add).then_inc(mix, 1)
                    dve.wait_ge(mix, q * 3 + 3)
                    v.tensor_tensor(tiles_of(y, q), new, diff, ALU.add).then_inc(y_ready, 1)
            pipeline(dve, tick, 1)

        @block.scalar
        def _(act):
            def tick(g):
                if group_live(g, 1):
                    q = g - 1
                    act.wait_ge(gates_psum, g)
                    wait(act, y_ready, q)
                    nc.scalar.activation(rz, gates[:, :, 0:2 * C], ACT.Sigmoid).then_inc(gates_ready, 1)
                    act.wait_ge(new_sum, g)
                    nc.scalar.activation(new, new, ACT.Tanh).then_inc(new_ready, 1)
                if group_live(g, 0):
                    act.wait_ge(turned, g + 1)
                    wait(act, gates_psum, g)
                    nc.scalar.copy(oT[0:C1, :], s.bank(TURN)[0:C1, :])
                    nc.scalar.copy(xT[0:C1, :], s.bank(TURN + 1)[0:C1, :]).then_inc(turned_back, 1)
            pipeline(act, tick, 1)

        @block.tensor
        def _(pe):
            t_ = nc.tensor
            pe.wait_ge(loaded, 64)
            pe.wait_ge(ones, 1)

            def tick(g):
                if group_live(g, 0):
                    pe.wait_ge(inputs_ready, g + 1)
                    wait(pe, turned_back, g)
                    turn_group(nc, s, o, s.bank(TURN), C1)
                    turn_group(nc, s, x, s.bank(TURN + 1), C1).then_inc(turned, 1)
                if group_live(g, 1):
                    pe.wait_ge(turned_back, g)
                    wait(pe, new_sum, g - 1)
                    for t in range(GRP):
                        to, at = s.bank(GATES, 2)[:, t * 4 * C:(t + 1) * 4 * C], slice(t * P, (t + 1) * P)
                        t_.matmul(to[:, 0:3 * C], oT[0:C1, at], Wih, start=True, stop=False)
                        t_.matmul(to[:, 0:2 * C], xT[0:C1, at], Whh[:, 0:2 * C], start=False, stop=True)
                        m = t_.matmul(to[:, 3 * C:4 * C], xT[0:C1, at], Whh[:, 2 * C:3 * C], start=True, stop=True)
                    m.then_inc(gates_psum, 1)
            pipeline(pe, tick, 1)
    layer_norm(nc, s, "pna_norm", y, square, s.Xv[:, :, 0:C])


def pass_scatter(nc, s, layer):
    tables = s.tables[layer]
    columns = s.arena[:, 0:3 * STEPS]
    target_col, weight_col = columns[:, 0:STEPS], columns[:, STEPS:2 * STEPS]
    scatter_row = columns[:, 2 * STEPS:3 * STEPS].bitcast(I32)
    wk = Carver(s.work)
    spread = wk.f32(2 * B4 * P).rearrange("p (r t n) -> p r t n", r=2, t=B4)
    same = wk.f32(4 * B4 * P).rearrange("p (r t n) -> p r t n", r=4, t=B4)
    weighted = wk.f32(2 * B4 * F).rearrange("p (r t f) -> p r t f", r=2, t=B4)
    merged = wk.f32(4 * B4 * F).rearrange("p (r t f) -> p r t f", r=4, t=B4)
    rels, targets = (wk.f32(ROUND * B4).rearrange("p (r t) -> p r t", r=ROUND) for _ in range(2))
    slots = wk.i32(ROUND * B4).rearrange("p (r t) -> p r t", r=ROUND)
    names = ("loaded", "released", "copied", "rels_turned", "targets_turned", "spread_ready", "same_ready", "x_psum",
             "weighted_ready", "merged_psum", "merged_ready", "rows_ready")
    (loaded, released, copied, rels_turned, targets_turned, spread_ready, same_ready, x_psum,
     weighted_ready, merged_psum, merged_ready, rows_ready) = (s.sem(f"scatter{layer}_{n}") for n in names)
    scattered = [s.sem(f"scatter{layer}_done{k}") for k in range(K)]
    REL, TARGET, X_BANK, MERGED = 0, 1, 2, 4
    CYCLE = K // B4

    def scatters(base, b):
        return (base + b) // CYCLE * 16 if isinstance(base, int) else base * (16 // CYCLE) + b // CYCLE * 16

    with nc.Block() as block:
        @block.sync
        def _(sp):
            sp.dma_start(columns, s.saved_cols).then_inc(loaded, 16)
            sp.wait_ge(loaded, 16)

        @block.gpsimd
        def _(pool):
            def tick(base, b):
                q = base + b
                pool.wait_ge(rows_ready, q + 1)
                pool.wait_ge(merged_ready, q + 1)
                for i in range(B4):
                    k = b % CYCLE * B4 + i
                    wait(pool, scattered[k], scatters(base, b))
                    pool.sem_inc(released, 1)
                    pool.indirect_dma_start(tables[k], bass.IndirectOffsetOnAxis(ap=slots[:, b, i:i + 1], axis=0),
                                            merged[:, b % 4, i, :], None, compute_op=ALU.add).then_inc(scattered[k], 16)
            rounds(pool, tick, 0)
            for k in range(K):
                pool.wait_ge(scattered[k], 16 * NB // CYCLE)

        @block.scalar
        def _(act):
            act.wait_ge(loaded, 16)

            def tick(base, b):
                if live(base, b, 0):
                    wait(act, same_ready, base + (b - 7))
                    nc.scalar.copy(rels[:, b, :], s.rel_col[:, steps4(base, b)])
                    nc.scalar.copy(targets[:, b, :], target_col[:, steps4(base, b)]).then_inc(copied, 1)
                if live(base, b, 4):
                    act.wait_ge(merged_psum, base + (b - 3))
                    for i in range(B4):
                        wait(act, scattered[b % CYCLE * B4 + i], scatters(base, b - 8 + CYCLE))
                    nc.scalar.copy(merged[:, b % 4], s.bank(MERGED + b % 2)[:, 0:B4 * F].rearrange("p (t f) -> p t f", t=B4))\
                        .then_inc(merged_ready, 1)
            rounds(act, tick, 4)

        @block.tensor
        def _(pe):
            js = [pe.alloc_register(f"scatter{layer}_tile{i}") for i in range(B4)]

            def tick(base, b):
                if live(base, b, 4):
                    q = base + (b - 4)
                    pe.wait_ge(weighted_ready, q + 1)
                    wait(pe, merged_ready, q - 1)
                    for i in range(B4):
                        m = nc.tensor.matmul(s.bank(MERGED + b % 2)[:, i * F:(i + 1) * F], same[:, b % 4, i, :],
                                             weighted[:, b % 2, i, :], start=True, stop=True)
                    m.then_inc(merged_psum, 1)
                if live(base, b, 2):
                    q = base + (b - 2)
                    pe.load(js, s.node_tile[0:1, steps4(base, b, 2)])
                    tiles = [pe.snap(pe.snap(j, min_val=0, max_val=NT - 1) * C1) for j in js]
                    pe.wait_ge(spread_ready, q + 1)
                    wait(pe, weighted_ready, q - 1)
                    for i in range(B4):
                        m = nc.tensor.matmul(s.bank(X_BANK + b % 2)[:, i * C1:(i + 1) * C1], spread[:, b % 2, i, :],
                                             s.X[:, bass.ds(tiles[i], C1)], start=True, stop=True)
                    m.then_inc(x_psum, 1)
                if live(base, b, 1):
                    q = base + (b - 1)
                    pe.wait_ge(copied, q + 1)
                    wait(pe, spread_ready, q)
                    for i in range(B4):
                        m = nc.tensor.transpose(s.bank(REL)[:, i * P:(i + 1) * P],
                                                rels[:, (b - 1) % ROUND, i:i + 1].broadcast_to((P, P)), s.ident[:, :])
                    m.then_inc(rels_turned, 1)
                    wait(pe, same_ready, q)
                    for i in range(B4):
                        m = nc.tensor.transpose(s.bank(TARGET)[:, i * P:(i + 1) * P],
                                                targets[:, (b - 1) % ROUND, i:i + 1].broadcast_to((P, P)), s.ident[:, :])
                    m.then_inc(targets_turned, 1)
            rounds(pe, tick, 4)

        @block.vector
        def _(dve):
            v = nc.vector
            v.memset(weighted[:, :, :, C1:F], 1.0)
            dve.wait_ge(loaded, 16)

            def tick(base, b):
                if live(base, b, 3):
                    q = base + (b - 3)
                    dve.wait_ge(x_psum, q + 1)
                    wait(dve, merged_psum, q - 1)
                    v.tensor_tensor(weighted[:, (b - 3) % 2, :, 0:C1],
                                    s.bank(X_BANK + (b - 3) % 2)[:, 0:B4 * C1].rearrange("p (t f) -> p t f", t=B4),
                                    weight_col[:, steps4(base, b, 3)].unsqueeze(2).broadcast_to((P, B4, C1)),
                                    ALU.mult).then_inc(weighted_ready, 1)
                if live(base, b, 1):
                    q = base + (b - 1)
                    dve.wait_ge(rels_turned, q + 1)
                    wait(dve, x_psum, q - 1)
                    v.tensor_scalar(spread[:, (b - 1) % 2], s.bank(REL).rearrange("p (t n) -> p t n", t=B4),
                                    s.iota_col[:, 0:1], None, ALU.is_equal).then_inc(spread_ready, 1)
                    dve.wait_ge(targets_turned, q + 1)
                    wait(dve, merged_psum, q - 3)
                    v.tensor_tensor(same[:, (b - 1) % 4], s.bank(TARGET).rearrange("p (t n) -> p t n", t=B4),
                                    targets[:, (b - 1) % ROUND, :].unsqueeze(2).broadcast_to((P, B4, P)),
                                    ALU.is_equal).then_inc(same_ready, 1)
                if live(base, b, 3):
                    wait(dve, merged_ready, base + (b - 6))
                    v.tensor_copy(slots[:, (b - 3) % ROUND, :], scatter_row[:, steps4(base, b, 3)]).then_inc(rows_ready, 1)
            rounds(dve, tick, 4)


def node_scatter(nc, s, A, layer):
    tables = s.tables[layer]
    K_IN = 2 * C if layer == 0 else C
    ar = Carver(s.arena)
    sums = ar.f32(NTP * F)
    y_at = ar.at
    y, square = (ar.f32(NTP * C).rearrange("p (j f) -> p j f", f=C) for _ in range(2))
    sums_v = sums.rearrange("p (j f) -> p j f", f=F)
    PARTS = 10
    M = NTP * F // PARTS
    loads = Carver(s.arena, y_at).f32(3 * K * M).rearrange("p (r k m) -> p r k m", r=3, k=K)
    wk = Carver(s.work)
    weight, bias = wk.f32(C)[0:K_IN, :], wk.f32(C)[0:1, :]
    inverse, share = wk.f32(NTP), wk.f32(NTP)
    R = max(K_IN, C1)
    rows = wk.f32(GRP * R).rearrange("p (t f) -> p t f", t=GRP)
    rowsT = wk.f32(GRP * P)
    names = ("weights_loaded", "summed", "steps", "rows_ready", "rows_turned", "rowsT_ready", "out_psum", "y_ready")
    (weights_loaded, summed, steps, rows_ready, rows_turned, rowsT_ready, out_psum, y_ready) = (
        s.sem(f"node{layer}_{n}") for n in names)
    loaded = [s.sem(f"node{layer}_loaded{r}") for r in range(3)]
    TURN, OUT = 0, 1
    over = lambda t: t.unsqueeze(2).broadcast_to((P, GRP, C))
    group_col = lambda t, g: t[:, bass.ds(g * GRP, GRP)]

    with nc.Block() as block:
        @block.sync
        def _(sp):
            sp.dma_start(weight, A["L2_gnn_weight" if layer == 0 else "L3_gnn_W"]).then_inc(weights_loaded, 16)
            sp.dma_start(bias, A["L2_gnn_bias" if layer == 0 else "L3_gnn_b"].unsqueeze(0)).then_inc(weights_loaded, 16)
            for a in range(PARTS):
                if a >= 3:
                    sp.wait_ge(summed, a - 2)
                for k in range(K):
                    sp.dma_start(loads[:, a % 3, k, :], tables[k].rearrange("(p r) f -> p (r f)", p=P)[:, a * M:(a + 1) * M])\
                        .then_inc(loaded[a % 3], 16)
            for r in range(3):
                sp.wait_ge(loaded[r], 16 * K * len(range(r, PARTS, 3)))
            sp.wait_ge(weights_loaded, 32)

        @block.vector
        def _(dve):
            v = nc.vector
            for a in range(PARTS):
                dve.wait_ge(loaded[a % 3], 16 * K * (a // 3 + 1))
                v.tensor_reduce(sums[:, a * M:(a + 1) * M], loads[:, a % 3].rearrange("p k m -> p m k"), AX_X, ALU.add)\
                    .then_inc(summed, 1)
            dve.wait_ge(summed, PARTS)
            if layer == 0:
                v.tensor_scalar(inverse, sums_v[:, :, C1], 1.0, None, ALU.max).then_inc(steps, 1)
                dve.wait_ge(steps, 1)
                v.reciprocal(inverse, inverse).then_inc(steps, 1)
                dve.wait_ge(steps, 2)
                v.tensor_tensor(share, sums_v[:, :, C], inverse, ALU.mult).then_inc(steps, 1)
                dve.wait_ge(steps, 3)

            def tick(g):
                if group_live(g, 0):
                    wait(dve, rows_turned, g)
                    if layer == 0:
                        v.tensor_tensor(rows[:, :, 0:C], tiles_of(s.Xv, g)[:, :, 0:C], over(group_col(share, g)), ALU.mult)
                        v.tensor_tensor(rows[:, :, C:2 * C], tiles_of(sums_v, g)[:, :, 0:C], over(group_col(inverse, g)),
                                        ALU.mult).then_inc(rows_ready, 1)
                    else:
                        v.tensor_copy(rows, tiles_of(sums_v, g)[:, :, 0:C1]).then_inc(rows_ready, 1)
                if group_live(g, 1):
                    dve.wait_ge(out_psum, g)
                    v.tensor_tensor(tiles_of(y, g - 1), s.bank(OUT)[:, 0:GRP * C].rearrange("p (t f) -> p t f", t=GRP),
                                    tiles_of(s.Xv, g - 1)[:, :, 0:C], ALU.add).then_inc(y_ready, 1)
            pipeline(dve, tick, 1)

        @block.scalar
        def _(act):
            def tick(g):
                if group_live(g, 0):
                    act.wait_ge(rows_turned, g + 1)
                    wait(act, out_psum, g)
                    nc.scalar.copy(rowsT[0:K_IN, :], s.bank(TURN)[0:K_IN, :]).then_inc(rowsT_ready, 1)
            pipeline(act, tick, 1)

        @block.tensor
        def _(pe):
            pe.wait_ge(weights_loaded, 32)

            def tick(g):
                if group_live(g, 0):
                    pe.wait_ge(rows_ready, g + 1)
                    wait(pe, rowsT_ready, g)
                    turn_group(nc, s, rows, s.bank(TURN), R).then_inc(rows_turned, 1)
                if group_live(g, 1):
                    pe.wait_ge(rowsT_ready, g)
                    wait(pe, y_ready, g - 1)
                    for t in range(GRP):
                        to = s.bank(OUT)[:, t * C:(t + 1) * C]
                        nc.tensor.matmul(to, s.ones_row[:, :], bias, start=True, stop=False)
                        m = nc.tensor.matmul(to, rowsT[0:K_IN, t * P:(t + 1) * P], weight, start=False, stop=True)
                    m.then_inc(out_psum, 1)
            pipeline(pe, tick, 1)

    layer_norm(nc, s, f"norm{layer}", y, square, s.Xv[:, :, 0:C])


def store(nc, s, out):
    stored = s.sem("stored")
    with nc.Block() as block:
        @block.sync
        def _(sp):
            sp.dma_start(out[0:(NT - 1) * P, :].rearrange("(j p) f -> p j f", p=P), s.Xv[:, 0:NT - 1, 0:C]).then_inc(stored, 16)
            sp.dma_start(out[(NT - 1) * P:N, :], s.Xv[0:N - (NT - 1) * P, NT - 1, 0:C]).then_inc(stored, 16)
            sp.wait_ge(stored, 32)


def phases(nc, s, A, out):
    with nc.cleanup_on_exit():
        prepare(nc, s, A)
        pass_gin(nc, s, A)
        node_gin(nc, s, A)
    with nc.cleanup_on_exit():
        messages_pna(nc, s, A)
        pass_pna(nc, s, A)
        node_pna_out(nc, s, A)
        node_pna_gru(nc, s, A)
    for layer in range(2):
        with nc.cleanup_on_exit():
            pass_scatter(nc, s, layer)
            node_scatter(nc, s, A, layer)
    with nc.cleanup_on_exit():
        store(nc, s, out)




def build(nc, A, out):
    with ExitStack() as ctx:
        s = Shared()

        def sb(name, shape, dt=F32):
            return ctx.enter_context(nc.sbuf_tensor(name, shape, dt))

        def dram(name, shape, dt=F32):
            return nc.dram_tensor(name, shape, dt, kind="Internal").ap()

        s.sem = lambda name: nc.alloc_semaphore(name=name)
        s.psum = ctx.enter_context(nc.psum_tensor("psum", [P, 8 * 512], F32))
        s.bank = lambda i, n=1: s.psum[:, 512 * i:512 * (i + n)]

        s.edge_rows = dram("edge_rows", (CH * P, NF * P))
        s.reset_rows = dram("reset_rows", (STEPS * P,), BF16)
        s.attr_rows = dram("attr_rows", (STEPS * 4, P))
        s.tile_list = dram("tile_list", (STEPS,), I32)
        s.message_table = dram("message_table", (P * NTP, C))
        s.x_saved = dram("x_saved", (P, NTP * C1))
        s.saved_cols = dram("saved_cols", (P, 3 * STEPS))
        s.tables = [[dram(f"sums{layer}_{k}", (P * NTP, F)) for k in range(K)] for layer in (2, 3)]

        s.X = sb("X", [P, NTP * C1])
        s.Xv = s.X[:, :].rearrange("p (j f) -> p j f", f=C1)
        s.message_row = sb("message_row", [P, STEPS], I32)
        s.rel_col = sb("rel_col", [P, STEPS])
        s.last_col = sb("last_col", [P, STEPS])
        s.ew_col = sb("ew_col", [P, STEPS])
        s.node_tile = sb("node_tile", [1, STEPS], U8)
        s.iota_row = sb("iota_row", [P, P])
        s.ident = sb("ident", [P, P])
        s.iota_col = sb("iota_col", [P, 1])
        s.dummy_col = sb("dummy_col", [P, 1])
        s.one_eps = sb("one_eps", [P, 1])
        s.eps_col = sb("eps_col", [P, 1])
        s.count = sb("count", [P, NTP])
        s.attr_weight = sb("attr_weight", [B4 * 4, B4 * C])
        s.ones_row = sb("ones_row", [1, P])
        s.arena = sb("arena", [P, NTP * 4 * C])
        s.work = sb("work", [P, 12900])

        wk = Carver(s.work)
        s.feature_row = wk.i32(STEPS)
        s.target_col = wk.f32(STEPS)
        s.weight_col = wk.f32(STEPS)
        s.scatter_row = wk.i32(STEPS)
        s.zeros = wk.f32(ZERO)
        s.pass0_at = wk.at
        phases(nc, s, A, out)


def kernel(**inputs):
    import numpy as _np
    import concourse.bacc as _bacc
    from concourse import mybir as _mybir
    from concourse.bass_utils import run_bass_kernel_spmd as _run

    nc = _bacc.Bacc("TRN2", target_bir_lowering=False, num_devices=1)
    arrays, args = {}, {}
    for name in INS:
        a = _np.ascontiguousarray(inputs[name])
        arrays[f"in_{name}_dram"] = a
        args[name] = nc.dram_tensor(f"in_{name}_dram", a.shape, _mybir.dt.from_np(a.dtype), kind="ExternalInput").ap()
    out = nc.dram_tensor("out_0_dram", (N, C), _mybir.dt.float32, kind="ExternalOutput").ap()
    build(nc, args, out)
    return _run(nc, [arrays], core_ids=[0]).results[0]["out_0_dram"]
```

```python
from contextlib import ExitStack

import concourse.bass as bass
from concourse import mybir

F32 = mybir.dt.float32
BF16 = mybir.dt.bfloat16
I32 = mybir.dt.int32
U8 = mybir.dt.uint8
ALU = mybir.AluOpType
ACT = mybir.ActivationFunctionType
AX_X = mybir.AxisListType.X

P = 128
N = 12500
E = 200000
C = 64
C1 = C + 1
HID = 128
NT = -(-N // P)
NTP = 100
DUMMY = NT
ET = -(-E // P)
B4 = 4
ROUND = 8
STEPS = -(-(ET + NT - 1) // (B4 * ROUND)) * B4 * ROUND
CH = STEPS // P
NB = STEPS // B4
ROUNDS = NB // ROUND
FULL = E // P
TAIL = E - FULL * P
FULLCH = FULL // P
REST = FULL - FULLCH * P
FAR = 1 << 20
NEG = -3.0e38
K = 8
F = C + 2
NF = 9
SRC, DST, FIRST, LAST, EW, W, EA = 0, 1, 2, 3, 4, 5, 6
EPS = 1e-5
GRP = 4
GROUPS = NTP // GRP
ZERO = 600

INS = ['x', 'src', 'dst', 'edge_attr_4', 'edge_weight', 'node_vec', 'L0_gnn_W1', 'L0_gnn_b1', 'L0_gnn_W2',
       'L0_gnn_b2', 'L0_gnn_eps', 'L1_gnn_W', 'L1_gnn_We', 'L1_gnn_be', 'L1_gnn_Wpre', 'L1_gnn_bpre',
       'L1_gnn_Wpost', 'L1_gnn_bpost', 'L1_gnn_Wih', 'L1_gnn_bih', 'L1_gnn_Whh', 'L1_gnn_bhh',
       'L2_gnn_weight', 'L2_gnn_bias', 'L3_gnn_W', 'L3_gnn_b']


class Shared:
    pass


class Carver:

    def __init__(self, tensor, at=0):
        self.t, self.at = tensor, at

    def f32(self, n):
        v = self.t[:, self.at:self.at + n]
        self.at += n
        assert self.at <= self.t.shape[1], (self.at, self.t.shape)
        return v

    def bf16(self, n):
        return self.f32(n // 2).bitcast(BF16)

    def i32(self, n):
        return self.f32(n).bitcast(I32)


def rounds(eng, tick, behind):
    for b in range(ROUND):
        tick(0, b)
    with eng.Fori(1, ROUNDS) as r:
        base = r * ROUND
        for b in range(ROUND):
            tick(base, b)
    for b in range(behind):
        tick(NB, b)


def live(base, b, lag):
    return not isinstance(base, int) or 0 <= base + b - lag < NB


def wait(eng, sem, value):
    if not isinstance(value, int) or value > 0:
        eng.wait_ge(sem, value)


def pipeline(eng, tick, depth, unroll=2):
    for g in range(4):
        tick(0, g)
    with eng.Fori(4 // unroll, GROUPS // unroll) as r:
        base = r * unroll
        for b in range(unroll):
            tick(base, b)
    for g in range(GROUPS // unroll * unroll, GROUPS + depth):
        tick(0, g)


def group_live(base, b, lag):
    return not isinstance(base, int) or 0 <= base + b - lag < GROUPS


def chain(eng, sem):
    n = [0]

    def done(op):
        n[0] += 1
        op.then_inc(sem, 1)
        eng.wait_ge(sem, n[0])
    return done


def prepare(nc, s, A):
    ar = Carver(s.arena)
    rows = ar.f32(CH * NF * P)
    rows_v = rows.rearrange("p (c f e) -> p c f e", c=CH, f=NF)
    scratch_at = ar.at
    raw_attr, raw_src, raw_dst = ar.f32(CH * 4 * P), ar.i32(CH * P), ar.i32(CH * P)
    raw_attr_v, raw_src_v, raw_dst_v = (t.rearrange("p (c e) -> p c e", c=CH) for t in (raw_attr, raw_src, raw_dst))
    wk = Carver(s.work, s.pass0_at)
    before_i, behind_i, last_tile_i, edge_tile_i, node_tile_i = (wk.i32(CH) for _ in range(5))
    before_f, behind_f, ends, edge_tile, node_tile_f, node_base, tile_no = (wk.f32(CH) for _ in range(7))
    ends_row, less = wk.f32(CH * P), wk.f32(CH * P)
    dummy_row, ones_edges, eps0 = wk.f32(P), wk.f32(P), wk.f32(1)
    tile_row_i = less.bitcast(I32)

    raw_clean, raw_loaded, consts, fields, edge_stored, by_step = (
        s.sem(n) for n in ("raw_clean", "raw_loaded", "consts", "fields", "edge_stored", "by_step"))
    ends_ready, ends_turned, step_work, tiles_ready, tiles_stored, tiles_loaded = (
        s.sem(n) for n in ("ends_ready", "ends_turned", "step_work", "tiles_ready", "tiles_stored", "tiles_loaded"))
    x_clean, x_loaded, eps_loaded = (s.sem(n) for n in ("x_clean", "x_loaded", "eps_loaded"))
    whole = FULLCH * P * P
    n_loads = 3 * 4 + 6

    def load_edges(eng, to, of, width):
        w = P * width
        eng.dma_start(to[:, 0:FULLCH, :], of[0:whole * width].rearrange("(c p e) -> p c e", p=P, e=w)).then_inc(raw_loaded, 16)
        eng.dma_start(to[0:REST, FULLCH, :], of[whole * width:FULL * w].rearrange("(p e) -> p e", e=w)).then_inc(raw_loaded, 16)
        eng.dma_start(to[REST:REST + 1, FULLCH, 0:TAIL * width],
                      of[FULL * w:E * width].rearrange("(p e) -> p e", p=1)).then_inc(raw_loaded, 16)

    with nc.Block() as block:
        @block.sync
        def _(sp):
            sp.wait_ge(raw_clean, 6)
            load_edges(sp, raw_dst_v, A["dst"], 1)
            load_edges(sp, raw_src_v, A["src"], 1)
            load_edges(sp, rows_v[:, :, W, :], A["edge_weight"], 1)
            load_edges(sp, raw_attr_v, A["edge_attr_4"].rearrange("e f -> (e f)"), 4)
            with nc.allow_non_contiguous_dma(reason="one number for each tile of 128 edges"):
                def one_per_tile(first, tiles):
                    return A["dst"][first:first + (tiles - 1) * P + 1:P]
                sp.dma_start(before_i[1:P, 0:1], one_per_tile(P - 1, P - 1).unsqueeze(1)).then_inc(raw_loaded, 16)
                sp.dma_start(before_i[:, 1:FULLCH], one_per_tile(P * P - 1, (FULLCH - 1) * P)
                             .rearrange("(c p) -> p c", p=P)).then_inc(raw_loaded, 16)
                sp.dma_start(before_i[0:REST + 1, FULLCH:CH], one_per_tile(whole - 1, REST + 1).unsqueeze(1)).then_inc(raw_loaded, 16)
                sp.dma_start(behind_i[:, 0:FULLCH], one_per_tile(P, FULLCH * P)
                             .rearrange("(c p) -> p c", p=P)).then_inc(raw_loaded, 16)
                sp.dma_start(behind_i[0:REST, FULLCH:CH], one_per_tile(whole + P, REST).unsqueeze(1)).then_inc(raw_loaded, 16)
                sp.dma_start(eps0, A["L0_gnn_eps"].partition_broadcast(P)).then_inc(raw_loaded, 16)
            sp.wait_ge(fields, 1)
            sp.dma_start(s.edge_rows.rearrange("(c p) f -> p c f", p=P),
                         rows.rearrange("p (c f) -> p c f", c=CH)).then_inc(edge_stored, 16)
            sp.wait_ge(tiles_ready, 1)
            with nc.allow_non_contiguous_dma(reason="one number for each step"):
                sp.dma_start(s.tile_list.rearrange("(c p) -> p c", p=P), node_tile_i).then_inc(tiles_stored, 16)
            sp.wait_ge(tiles_stored, 16)
            sp.dma_start(tile_row_i[0:1, :], s.tile_list.rearrange("(a n) -> a n", a=1)).then_inc(tiles_loaded, 16)
            sp.wait_ge(tiles_loaded, 16)
            sp.wait_ge(edge_stored, 16)

        @block.scalar
        def _(act):
            act.wait_ge(x_clean, 2)
            act.wait_ge(raw_loaded, 16 * n_loads)
            act.dma_start(s.Xv[:, 0:NT - 1, 0:C], A["x"][0:(NT - 1) * P, :].rearrange("(j p) f -> p j f", p=P)).then_inc(x_loaded, 16)
            act.dma_start(s.Xv[0:N - (NT - 1) * P, NT - 1, 0:C], A["x"][(NT - 1) * P:N, :]).then_inc(x_loaded, 16)
            act.wait_ge(x_loaded, 32)

        @block.gpsimd
        def _(pool):
            def numbers(to, pattern, base, by_partition):
                nc.gpsimd.iota(to, pattern=pattern, base=base, channel_multiplier=by_partition,
                               allow_small_or_imprecise_dtypes=True).then_inc(consts, 1)
            numbers(s.iota_row[:, :], [[1, P]], 0, 0)
            numbers(s.iota_col[:, :], [[0, 1]], 0, 1)
            numbers(tile_no, [[P, CH]], 0, 1)
            numbers(dummy_row, [[NTP, P]], DUMMY, 0)
            numbers(s.dummy_col[:, :], [[0, 1]], DUMMY, NTP)
            nc.gpsimd.memset(s.ident[:, :], 1.0).then_inc(consts, 1)
            pool.wait_ge(consts, 6)
            nc.gpsimd.affine_select(out=s.ident[:, :], in_=s.ident[:, :], compare_op=ALU.is_equal, fill=0.0,
                                    base=0, pattern=[[-1, P]], channel_multiplier=1).then_inc(consts, 1)
            pool.wait_ge(edge_stored, 16)
            pool.wait_ge(tiles_ready, 1)
            for c in range(CH):
                pool.indirect_dma_start(rows[:, c * NF * P:(c + 1) * NF * P], None, s.edge_rows,
                                        bass.IndirectOffsetOnAxis(ap=edge_tile_i[:, c:c + 1], axis=0)).then_inc(by_step, 16)
            pool.wait_ge(by_step, 16 * CH)

        @block.tensor
        def _(pe):
            pe.wait_ge(consts, 7)
            pe.wait_ge(ends_ready, 1)
            for c in range(CH):
                pe.transpose(s.psum[:, c * P:(c + 1) * P], ends[:, c:c + 1].broadcast_to((P, P)),
                             s.ident[:, :]).then_inc(ends_turned, 1)

        @block.vector
        def _(dve):
            done = chain(dve, step_work)
            v = nc.vector
            v.memset(raw_src_v[:, CH - 1, :], 0).then_inc(raw_clean, 1)
            v.memset(raw_dst_v[:, CH - 1, :], FAR).then_inc(raw_clean, 1)
            v.memset(raw_attr_v[:, CH - 1, :], 0.0).then_inc(raw_clean, 1)
            v.memset(rows_v[:, CH - 1, W, :], 0.0).then_inc(raw_clean, 1)
            v.memset(before_i, -1).then_inc(raw_clean, 1)
            v.memset(behind_i, FAR).then_inc(raw_clean, 1)
            v.memset(s.Xv[:, :, 0:C], 0.0).then_inc(x_clean, 1)
            v.memset(s.Xv[:, :, C:C1], 1.0).then_inc(x_clean, 1)
            v.memset(s.zeros, 0.0)
            v.memset(s.ones_row[:, :], 1.0)
            v.memset(ones_edges, 1.0)
            done(v.memset(s.eps_col[:, :], EPS))
            dve.wait_ge(raw_loaded, 16 * n_loads)
            done(v.tensor_scalar(s.one_eps[:, :], eps0, 1.0, None, ALU.add))
            done(v.tensor_copy(rows_v[:, :, DST, :], raw_dst_v))
            v.tensor_copy(rows_v[:, :, SRC, :], raw_src_v)
            v.tensor_copy(before_f, before_i)
            done(v.tensor_copy(behind_f, behind_i))
            D = rows_v[:, :, DST, :]
            v.tensor_tensor(rows_v[:, :, FIRST, 1:P], D[:, :, 1:P], D[:, :, 0:P - 1], ALU.not_equal)
            v.tensor_tensor(rows_v[:, :, FIRST, 0], D[:, :, 0], before_f, ALU.not_equal)
            v.tensor_tensor(rows_v[:, :, LAST, 0:P - 1], D[:, :, 1:P], D[:, :, 0:P - 1], ALU.not_equal)
            v.tensor_tensor(rows_v[:, :, LAST, P - 1], D[:, :, P - 1], behind_f, ALU.not_equal)
            by_edge = raw_attr.rearrange("p (c e f) -> p c e f", c=CH, f=4)
            v.tensor_copy(rows_v[:, :, EW, :], by_edge[:, :, :, 3])
            for f in range(3):
                last = v.tensor_copy(rows_v[:, :, EA + f, :], by_edge[:, :, :, f])
            done(last)
            v.engine_nop().then_inc(fields, 1)
            done(v.tensor_scalar(last_tile_i, raw_dst_v[:, :, P - 1], 7, None, ALU.logical_shift_right))
            done(v.tensor_copy(ends, last_tile_i))
            dve.wait_ge(consts, 7)
            done(v.tensor_tensor(ends, ends, tile_no, ALU.add))
            v.engine_nop().then_inc(ends_ready, 1)
            dve.wait_ge(ends_turned, CH)
            done(v.tensor_copy(ends_row, s.psum[:, 0:CH * P]))
            for c in range(CH):
                done(v.tensor_scalar(less, ends_row, tile_no[:, c:c + 1], 0.0, ALU.is_lt, ALU.add, accum_out=edge_tile[:, c:c + 1]))
            done(v.tensor_tensor(node_tile_f, tile_no, edge_tile, ALU.subtract))
            done(v.tensor_scalar(node_base, node_tile_f, float(P), None, ALU.mult))
            done(v.tensor_scalar(node_tile_f, node_tile_f, float(NT - 1), None, ALU.min))
            v.tensor_copy(node_tile_i, node_tile_f)
            done(v.tensor_copy(edge_tile_i, edge_tile))
            v.engine_nop().then_inc(tiles_ready, 1)
            dve.wait_ge(tiles_loaded, 16)
            done(v.tensor_copy(s.node_tile[:, :], tile_row_i[0:1, :]))

    ar = Carver(s.arena, scratch_at)
    src_i, low, high = ar.i32(CH * P), ar.i32(CH * P), ar.i32(CH * P)
    table_row, member, target = ar.f32(CH * P), ar.f32(CH * P), ar.f32(CH * P)
    reset = src_i.bitcast(BF16)[:, 0:CH * P]
    row3 = lambda t: t.rearrange("p (c e) -> p c e", c=CH)
    row_work, resets_ready, rows_out, columns = (s.sem(n) for n in ("row_work", "resets_ready", "rows_out", "columns"))
    field_ready, turned = s.sem("field_ready"), s.sem("turned")
    cols = [(rows_v[:, :, SRC, :], s.feature_row), (row3(table_row), s.message_row[:, :]), (row3(target), s.target_col),
            (rows_v[:, :, DST, :], s.rel_col[:, :]), (rows_v[:, :, LAST, :], s.last_col[:, :]),
            (rows_v[:, :, EW, :], s.ew_col[:, :]), (rows_v[:, :, W, :], s.weight_col)]
    parts = [(a, min(B4, CH - a)) for a in range(0, CH, B4)]

    with nc.Block() as block:
        @block.vector
        def _(dve):
            done = chain(dve, row_work)
            v = nc.vector
            R = rows_v
            by_row = lambda t: t.unsqueeze(1).broadcast_to((P, CH, P))
            v.tensor_tensor(R[:, :, DST, :], R[:, :, DST, :], node_base.unsqueeze(2).broadcast_to((P, CH, P)), ALU.subtract)
            done(v.tensor_copy(row3(src_i), R[:, :, SRC, :]))
            v.tensor_scalar(low, src_i, P - 1, None, ALU.bitwise_and)
            done(v.tensor_scalar(high, src_i, 7, None, ALU.logical_shift_right))
            v.tensor_scalar(row3(reset), R[:, :, FIRST, :], NEG, None, ALU.mult).then_inc(resets_ready, 1)
            v.tensor_scalar(member, low, float(NTP), None, ALU.mult)
            v.tensor_copy(target, high)
            done(v.engine_nop())
            done(v.tensor_tensor(table_row, member, target, ALU.add))
            v.tensor_scalar(row3(member), R[:, :, DST, :], 0.0, None, ALU.is_ge)
            v.tensor_scalar(row3(target), R[:, :, DST, :], float(P), None, ALU.is_lt)
            done(v.engine_nop())
            done(v.tensor_tensor(member, member, target, ALU.mult))
            done(v.tensor_tensor(row3(target), row3(table_row), by_row(dummy_row), ALU.subtract))
            done(v.tensor_tensor(target, target, member, ALU.mult))
            done(v.tensor_tensor(row3(target), row3(target), by_row(dummy_row), ALU.add))
            v.engine_nop().then_inc(field_ready, 1)
            n = 0
            for _, to in cols:
                for a, m in parts:
                    n += 1
                    dve.wait_ge(turned, n)
                    v.tensor_copy(to[:, a * P:(a + m) * P], s.bank(n % 2)[:, 0:m * P]).then_inc(columns, 1)

        @block.tensor
        def _(pe):
            pe.wait_ge(field_ready, 1)
            n = 0
            for of, _ in cols:
                for a, m in parts:
                    n += 1
                    if n > 2:
                        pe.wait_ge(columns, n - 2)
                    for c in range(m):
                        t = pe.transpose(s.bank(n % 2)[:, c * P:(c + 1) * P], of[:, a + c, :], s.ident[:, :])
                    t.then_inc(turned, 1)

        @block.sync
        def _(sp):
            sp.wait_ge(resets_ready, 1)
            sp.dma_start(s.reset_rows.rearrange("(c p e) -> p c e", p=P, e=P), row3(reset)).then_inc(rows_out, 16)
            attr_rows = s.attr_rows.rearrange("(c p f) e -> p c f e", p=P, f=4)
            for f in range(3):
                sp.dma_start(attr_rows[:, :, f, :], rows_v[:, :, EA + f, :]).then_inc(rows_out, 16)
            sp.dma_start(attr_rows[:, :, 3, :],
                         ones_edges.unsqueeze(1).broadcast_to((P, CH, P))).then_inc(rows_out, 16)
            sp.wait_ge(rows_out, 16 * 5)


def gather_rows(pool, s, table, ring_rows, slots, landed, rows_ready, free, released):
    def tick(base, b):
        wait(pool, rows_ready, base + b + 1)
        wait(pool, free, base + b - 3)
        pool.sem_inc(released, 1)
        for i in range(B4):
            pool.indirect_dma_start(ring_rows(b % 4, i), None, table,
                                    bass.IndirectOffsetOnAxis(ap=slots[:, b, i:i + 1], axis=0)).then_inc(landed[b % 4], 16)
    rounds(pool, tick, 0)
    for k in range(4):
        pool.wait_ge(landed[k], 16 * B4 * (NB // 4))


def steps4(base, b, lag=0):
    return bass.ds((base + (b - lag)) * B4, B4)


def pass_gin(nc, s, A):
    wk = Carver(s.work, s.pass0_at)
    onehot = wk.f32(2 * B4 * P).rearrange("p (r t n) -> p r t n", r=2, t=B4)
    ring = wk.f32(4 * B4 * C1).rearrange("p (r t f) -> p r t f", r=4, t=B4)
    slots = wk.i32(ROUND * B4).rearrange("p (r t) -> p r t", r=ROUND)
    targets = wk.f32(ROUND * B4).rearrange("p (r t) -> p r t", r=ROUND)
    same = wk.f32(B4 * P).rearrange("p (t n) -> p t n", t=B4)
    before = wk.f32(P)
    repeats = wk.f32(STEPS)
    sums = s.arena[:, 0:NTP * C1]
    sums_v = sums.rearrange("p (j f) -> p j f", f=C1)
    landed = [s.sem(f"gin_landed{k}") for k in range(4)]
    rows_ready, onehot_ready, part_ready, added, released = (
        s.sem("gin_" + n) for n in ("rows_ready", "onehot_ready", "part_ready", "added", "released"))
    targets_turned, same_ready, masked, repeats_ready, saved, cleared = (
        s.sem("gin_" + n) for n in ("targets_turned", "same_ready", "masked", "repeats_ready", "saved", "cleared"))
    last_work, counted, targets_ready = s.sem("gin_last_work"), s.sem("gin_counted"), s.sem("gin_targets_ready")
    PART, TURN = 0, 2

    with nc.Block() as block:
        @block.gpsimd
        def _(pool):
            gather_rows(pool, s, A["x"], lambda r, i: ring[:, r, i, 0:C], slots, landed, rows_ready, part_ready, released)

        @block.sync
        def _(sp):
            for n, layer in enumerate(s.tables):
                for k, table in enumerate(layer):
                    sp.wait_ge(part_ready, (n * K + k + 1) * (NB // (2 * K + 2)))
                    sp.dma_start(table.rearrange("(p r) f -> p (r f)", p=P).rearrange("p (n m) -> p n m", m=ZERO),
                                 s.zeros.unsqueeze(1).broadcast_to((P, NTP * F // ZERO, ZERO))).then_inc(cleared, 16)
            sp.wait_ge(cleared, 16 * 2 * K)
            sp.wait_ge(repeats_ready, 1)
            for n, t in enumerate((s.target_col, s.weight_col, s.scatter_row.bitcast(F32))):
                sp.dma_start(s.saved_cols[:, n * STEPS:(n + 1) * STEPS], t).then_inc(saved, 16)
            sp.wait_ge(saved, 16 * 3)

        @block.tensor
        def _(pe):
            def tick(base, b):
                if live(base, b, 1):
                    q = base + (b - 1)
                    pe.wait_ge(onehot_ready, q + 1)
                    pe.wait_ge(landed[(b - 1) % 4], landings(base, b - 1))
                    wait(pe, added, B4 * q - B4)
                    o = s.bank(PART + (b - 1) % 2)
                    for i in range(B4):
                        m = nc.tensor.matmul(o[:, i * C1:(i + 1) * C1], onehot[:, (b - 1) % 2, i, :],
                                             ring[:, (b - 1) % 4, i, :], start=True, stop=True)
                    m.then_inc(part_ready, 1)
                if live(base, b, 0):
                    pe.wait_ge(targets_ready, base + (b + 1))
                    wait(pe, same_ready, base + b)
                    for i in range(B4):
                        m = nc.tensor.transpose(s.bank(TURN)[:, i * P:(i + 1) * P],
                                                targets[:, b, i:i + 1].broadcast_to((P, P)), s.ident[:, :])
                    m.then_inc(targets_turned, 1)
            rounds(pe, tick, 1)

        @block.scalar
        def _(act):
            def tick(base, b):
                wait(act, same_ready, base + (b - 7))
                nc.scalar.copy(targets[:, b, :], s.target_col[:, steps4(base, b)]).then_inc(targets_ready, 1)
            rounds(act, tick, 0)

        @block.vector
        def _(dve):
            v = nc.vector
            v.memset(sums, 0.0).then_inc(added, B4)
            v.memset(ring[:, :, :, C:C1], 1.0)
            v.tensor_scalar(before, s.iota_row[:, :], s.iota_col[:, 0:1], None, ALU.is_lt)
            js = [dve.alloc_register(f"gin_tile{i}") for i in range(B4)]

            def tick(base, b):
                if live(base, b, 0):
                    wait(dve, part_ready, base + (b - 7))
                    v.tensor_copy(slots[:, b, :], s.feature_row[:, steps4(base, b)]).then_inc(rows_ready, 1)
                lag = 4
                if live(base, b, lag):
                    wait(dve, part_ready, base + (b - lag - 1))
                    v.tensor_tensor(onehot[:, b % 2], s.iota_row[:, :].unsqueeze(1).broadcast_to((P, B4, P)),
                                    s.rel_col[:, steps4(base, b, lag)].unsqueeze(2).broadcast_to((P, B4, P)),
                                    ALU.is_equal).then_inc(onehot_ready, 1)
                if live(base, b, lag + 1):
                    q = base + (b - lag - 1)
                    dve.load(js, s.node_tile[0:1, steps4(base, b, lag + 1)])
                    tiles = [dve.snap(dve.snap(j, min_val=0, max_val=NT - 1) * C1) for j in js]
                    dve.wait_ge(part_ready, q + 1)

                def add(i):
                    if live(base, b, lag + 1):
                        dve.wait_ge(added, q * B4 + (B4 + i))
                        to = sums[:, bass.ds(tiles[i], C1)]
                        part = s.bank(PART + (b - 1) % 2)[:, i * C1:(i + 1) * C1]
                        v.tensor_tensor(to, part, to, ALU.add).then_inc(added, 1)

                add(0)
                if live(base, b, lag):
                    q0 = base + (b - lag)
                    dve.wait_ge(targets_turned, q0 + 1)
                    wait(dve, counted, q0)
                    v.tensor_tensor(same, s.bank(TURN).rearrange("p (t n) -> p t n", t=B4),
                                    targets[:, (b - lag) % ROUND, :].unsqueeze(2).broadcast_to((P, B4, P)),
                                    ALU.is_equal).then_inc(same_ready, 1)
                add(1)
                if live(base, b, lag):
                    dve.wait_ge(same_ready, q0 + 1)
                    v.tensor_tensor(same, same, before.unsqueeze(1).broadcast_to((P, B4, P)), ALU.mult).then_inc(masked, 1)
                add(2)
                if live(base, b, lag):
                    dve.wait_ge(masked, q0 + 1)
                    v.tensor_reduce(repeats[:, steps4(base, b, lag)], same, AX_X, ALU.add).then_inc(counted, 1)
                add(3)

            rounds(dve, tick, 5)
            done = chain(dve, last_work)
            dve.wait_ge(counted, NB)
            dve.wait_ge(added, B4 * (NB + 1))
            target = same.rearrange("p t n -> p (t n)")
            for a in range(0, STEPS, B4 * P):
                m = min(B4 * P, STEPS - a)
                done(v.tensor_scalar(target[:, 0:m], s.target_col[:, a:a + m], s.dummy_col[:, 0:1], None, ALU.subtract))
                done(v.scalar_tensor_tensor(out=target[:, 0:m], in0=repeats[:, a:a + m], scalar=0.0, in1=target[:, 0:m],
                                            op0=ALU.is_equal, op1=ALU.mult))
                done(v.tensor_scalar(s.scatter_row[:, a:a + m], target[:, 0:m], s.dummy_col[:, 0:1], None, ALU.add))
            done(v.tensor_copy(s.count[:, :], sums_v[:, :, C]))
            v.engine_nop().then_inc(repeats_ready, 1)


def landings(base, b):
    return (base // 4 + (b // 4 + 1)) * (16 * B4) if isinstance(base, int) else base * (4 * B4) + (b // 4 + 1) * (16 * B4)


def layer_norm(nc, s, name, y, square, to, out=None):
    parts = 4
    m = NTP // parts
    wk = Carver(s.work, s.work.shape[1] - 3 * NTP)
    total, spread, scale = wk.f32(NTP), wk.f32(NTP), wk.f32(NTP)
    centred, squared, deviation, steps = (s.sem(f"{name}_{n}") for n in ("centred", "squared", "deviation", "norm_steps"))
    spread_ready, normed, stored = (s.sem(f"{name}_{n}") for n in ("spread_ready", "normed", "stored"))
    over = lambda t: t.unsqueeze(2).broadcast_to((P, m, C))

    with nc.Block() as block:
        @block.vector
        def _(dve):
            v = nc.vector
            at = [slice(k * m, (k + 1) * m) for k in range(parts)]
            for k in range(parts):
                v.tensor_reduce(total[:, at[k]], y[:, at[k], :], AX_X, ALU.add).then_inc(steps, 1)
                dve.wait_ge(steps, 2 * k + 1)
                v.tensor_scalar(total[:, at[k]], total[:, at[k]], 1.0 / C, None, ALU.mult).then_inc(steps, 1)
                dve.wait_ge(steps, 2 * k + 2)
                v.tensor_tensor(y[:, at[k], :], y[:, at[k], :], over(total[:, at[k]]), ALU.subtract).then_inc(centred, 1)
            for k in range(parts):
                dve.wait_ge(squared, k + 1)
                v.tensor_reduce(spread[:, at[k]], square[:, at[k], :], AX_X, ALU.add).then_inc(spread_ready, 1)
            for k in range(parts):
                dve.wait_ge(deviation, k + 1)
                v.reciprocal(scale[:, at[k]], spread[:, at[k]]).then_inc(steps, 1)
                dve.wait_ge(steps, 2 * parts + k + 1)
                dve.wait_ge(centred, k + 1)
                v.tensor_tensor(to[:, at[k], :], y[:, at[k], :], over(scale[:, at[k]]), ALU.mult).then_inc(normed, 1)

        @block.sync
        def _(sp):
            if out is not None:
                for k in range(parts):
                    a, z = k * m, min((k + 1) * m, NT - 1)
                    sp.wait_ge(normed, k + 1)
                    sp.dma_start(out[a * P:z * P, :].rearrange("(j p) f -> p j f", p=P), to[:, a:z, :]).then_inc(stored, 16)
                sp.dma_start(out[(NT - 1) * P:N, :], to[0:N - (NT - 1) * P, NT - 1, :]).then_inc(stored, 16)
                sp.wait_ge(stored, 16 * (parts + 1))

        @block.scalar
        def _(act):
            at = [slice(k * m, (k + 1) * m) for k in range(parts)]
            for k in range(parts):
                act.wait_ge(centred, k + 1)
                nc.scalar.activation(square[:, at[k], :], y[:, at[k], :], ACT.Square).then_inc(squared, 1)
            for k in range(parts):
                act.wait_ge(spread_ready, k + 1)
                nc.scalar.activation(spread[:, at[k]], spread[:, at[k]], ACT.Sqrt, bias=s.eps_col[:, 0:1],
                                     scale=1.0 / C).then_inc(deviation, 1)


def tiles_of(view, g):
    return view[:, bass.ds(g * GRP, GRP), :]


def turn_group(nc, s, of, to, rows):
    for t in range(GRP):
        ins = nc.tensor.transpose(to[0:rows, t * P:(t + 1) * P], of[:, t, 0:rows], s.ident[:, :])
    return ins


def node_gin(nc, s, A):
    sums = s.arena[:, 0:NTP * C1].rearrange("p (j f) -> p j f", f=C1)
    ar = Carver(s.arena, NTP * C1)
    y, square = (ar.f32(NTP * C).rearrange("p (j f) -> p j f", f=C) for _ in range(2))
    wk = Carver(s.work)
    W1, b1, W2, b2 = wk.f32(HID)[0:C, :], wk.f32(1), wk.f32(C), wk.f32(GRP * C)[0:1, :]
    hT, hidden = (wk.f32(2 * GRP * P).rearrange("p (r n) -> p r n", r=2) for _ in range(2))
    h = wk.f32(2 * GRP * C1).rearrange("p (r t f) -> p r t f", r=2, t=GRP)
    loaded, h_ready, hT_psum, hT_ready, hidden_psum, hidden_ready, out_psum, y_ready = (
        s.sem("gin_node_" + n) for n in ("loaded", "h_ready", "hT_psum", "hT_ready", "hidden_psum", "hidden_ready",
                                         "out_psum", "y_ready"))
    TURN, HIDDEN, OUT = 0, 2, 4

    with nc.Block() as block:
        @block.sync
        def _(sp):
            sp.dma_start(W1, A["L0_gnn_W1"]).then_inc(loaded, 16)
            sp.dma_start(W2, A["L0_gnn_W2"]).then_inc(loaded, 16)
            for t in range(GRP):
                sp.dma_start(b2[:, t * C:(t + 1) * C], A["L0_gnn_b2"].unsqueeze(0)).then_inc(loaded, 16)
            with nc.allow_non_contiguous_dma(reason="a bias by partition"):
                sp.dma_start(b1, A["L0_gnn_b1"].unsqueeze(1)).then_inc(loaded, 16)
            sp.wait_ge(loaded, 16 * (3 + GRP))

        @block.vector
        def _(dve):
            v = nc.vector

            def tick(base, b):
                if group_live(base, b, 0):
                    g = base + b
                    wait(dve, hT_psum, g - 1)
                    v.scalar_tensor_tensor(out=h[:, b % 2], in0=tiles_of(s.Xv, g), scalar=s.one_eps[:, 0:1],
                                           in1=tiles_of(sums, g), op0=ALU.mult, op1=ALU.add).then_inc(h_ready, 1)
                if group_live(base, b, 3):
                    g = base + (b - 3)
                    dve.wait_ge(out_psum, g + 1)
                    v.tensor_tensor(tiles_of(y, g), s.bank(OUT + (b - 3) % 2)[:, 0:GRP * C].rearrange("p (t f) -> p t f", t=GRP),
                                    tiles_of(s.Xv, g)[:, :, 0:C], ALU.add).then_inc(y_ready, 1)
            pipeline(dve, tick, 3)

        @block.scalar
        def _(act):
            act.wait_ge(loaded, 16 * (3 + GRP))

            def tick(base, b):
                if group_live(base, b, 0):
                    g = base + b
                    act.wait_ge(hT_psum, g + 1)
                    wait(act, hidden_psum, g - 1)
                    nc.scalar.copy(hT[0:C, b % 2], s.bank(TURN + b % 2)[0:C, :]).then_inc(hT_ready, 1)
                if group_live(base, b, 1):
                    g = base + (b - 1)
                    act.wait_ge(hidden_psum, g + 1)
                    wait(act, out_psum, g - 1)
                    nc.scalar.activation(hidden[:, (b - 1) % 2], s.bank(HIDDEN + (b - 1) % 2), ACT.Relu, bias=b1[:, 0:1])\
                        .then_inc(hidden_ready, 1)
            pipeline(act, tick, 1)

        @block.tensor
        def _(pe):
            pe.wait_ge(loaded, 16 * (3 + GRP))

            def tick(base, b):
                if group_live(base, b, 0):
                    g = base + b
                    pe.wait_ge(h_ready, g + 1)
                    wait(pe, hT_ready, g - 1)
                    turn_group(nc, s, h[:, b % 2], s.bank(TURN + b % 2), C1).then_inc(hT_psum, 1)
                if group_live(base, b, 1):
                    g = base + (b - 1)
                    pe.wait_ge(hT_ready, g + 1)
                    wait(pe, hidden_ready, g - 1)
                    nc.tensor.matmul(s.bank(HIDDEN + (b - 1) % 2), W1, hT[0:C, (b - 1) % 2], start=True, stop=True)\
                        .then_inc(hidden_psum, 1)
                if group_live(base, b, 2):
                    g = base + (b - 2)
                    pe.wait_ge(hidden_ready, g + 1)
                    wait(pe, y_ready, g - 1)
                    to = s.bank(OUT + b % 2)
                    nc.tensor.matmul(to[:, 0:GRP * C], s.ones_row[:, :], b2, start=True, stop=False)
                    for t in range(GRP):
                        m = nc.tensor.matmul(to[:, t * C:(t + 1) * C], hidden[:, b % 2, t * P:(t + 1) * P], W2,
                                             start=False, stop=t == GRP - 1)
                    m.then_inc(out_psum, 1)
            pipeline(pe, tick, 2)
    layer_norm(nc, s, "gin_norm", y, square, s.Xv[:, :, 0:C])


def messages_pna(nc, s, A):
    wk = Carver(s.work)
    stack, Wpre = wk.f32(C), wk.f32(3 * C)[0:C, :].rearrange("p (k f) -> p k f", k=3)
    stackT, both = wk.f32(C + 4)[0:C, :], wk.f32(2 * C)[0:C, :]
    x = wk.f32(2 * GRP * C1).rearrange("p (r t f) -> p r t f", r=2, t=GRP)
    xT = wk.f32(2 * GRP * P).rearrange("p (r n) -> p r n", r=2)
    attr_weight = wk.f32(C)[0:4, :]
    by_src = s.arena[:, 0:NTP * C].rearrange("p (j f) -> p j f", f=C)
    loaded, stack_turned, stack_ready, products, weights_ready, kept, stored = (
        s.sem("msg_" + n) for n in ("loaded", "stack_turned", "stack_ready", "products", "weights_ready", "kept", "stored"))
    x_ready, xT_psum, xT_ready, out_psum, dst_ready, src_ready = (
        s.sem("msg_" + n) for n in ("x_ready", "xT_psum", "xT_ready", "out_psum", "dst_ready", "src_ready"))
    placed = s.sem("msg_placed")
    TURN, OUT, SMALL = 0, 2, 4
    R = C + 4

    with nc.Block() as block:
        @block.sync
        def _(sp):
            sp.dma_start(stack[0:C, :], A["L1_gnn_W"]).then_inc(loaded, 16)
            sp.dma_start(stack[C:C + 3, :], A["L1_gnn_We"]).then_inc(loaded, 16)
            sp.dma_start(stack[C + 3:R, :], A["L1_gnn_be"].unsqueeze(0)).then_inc(loaded, 16)
            sp.dma_start(Wpre, A["L1_gnn_Wpre"].rearrange("(k p) f -> p k f", p=C)).then_inc(loaded, 16)
            sp.dma_start(s.x_saved, s.X[:, :]).then_inc(kept, 16)
            sp.wait_ge(weights_ready, 2)
            for i in range(B4):
                sp.dma_start(s.attr_weight[i * 4:(i + 1) * 4, i * C:(i + 1) * C], attr_weight).then_inc(placed, 16)
            sp.wait_ge(placed, 16 * B4)
            sp.wait_ge(src_ready, GROUPS)
            sp.dma_start(s.message_table.rearrange("(p r) f -> p (r f)", p=P), s.arena[:, 0:NTP * C]).then_inc(stored, 16)
            sp.wait_ge(stored, 16)

        @block.tensor
        def _(pe):
            pe.wait_ge(loaded, 64)
            nc.tensor.transpose(s.bank(SMALL)[0:C, 0:R], stack[0:R, :], s.ident[0:R, 0:R]).then_inc(stack_turned, 1)
            pe.wait_ge(stack_ready, 1)
            nc.tensor.matmul(s.bank(SMALL)[0:C, 0:C], stackT[:, 0:C], Wpre[:, 1, :], start=True, stop=True)
            nc.tensor.matmul(s.bank(SMALL)[0:C, C:2 * C], stackT[:, 0:C], Wpre[:, 0, :], start=True, stop=True)
            nc.tensor.matmul(s.bank(SMALL)[0:4, 2 * C:3 * C], stackT[:, C:R], Wpre[:, 2, :], start=True, stop=True).then_inc(products, 1)
            pe.wait_ge(weights_ready, 2)

            def tick(base, b):
                if group_live(base, b, 0):
                    g = base + b
                    pe.wait_ge(x_ready, g + 1)
                    wait(pe, xT_ready, g - 1)
                    turn_group(nc, s, x[:, b % 2], s.bank(TURN + b % 2), C1).then_inc(xT_psum, 1)
                if group_live(base, b, 1):
                    g = base + (b - 1)
                    pe.wait_ge(xT_ready, g + 1)
                    wait(pe, src_ready, g - 1)
                    for t in range(GRP):
                        m = nc.tensor.matmul(s.bank(OUT + (b - 1) % 2)[:, t * 2 * C:(t + 1) * 2 * C],
                                             xT[0:C, (b - 1) % 2, t * P:(t + 1) * P], both, start=True, stop=True)
                    m.then_inc(out_psum, 1)
            pipeline(pe, tick, 1)

        @block.vector
        def _(dve):
            v = nc.vector
            dve.wait_ge(stack_turned, 1)
            v.tensor_copy(stackT, s.bank(SMALL)[0:C, 0:R]).then_inc(stack_ready, 1)
            dve.wait_ge(products, 1)
            v.tensor_copy(both, s.bank(SMALL)[0:C, 0:2 * C]).then_inc(weights_ready, 1)
            v.memset(s.attr_weight[:, :], 0.0)
            v.tensor_copy(attr_weight, s.bank(SMALL)[0:4, 2 * C:3 * C]).then_inc(weights_ready, 1)
            dve.wait_ge(kept, 16)

            def tick(base, b):
                if group_live(base, b, 0):
                    g = base + b
                    wait(dve, xT_psum, g - 1)
                    v.tensor_copy(x[:, b % 2], tiles_of(s.Xv, g)).then_inc(x_ready, 1)
                if group_live(base, b, 2):
                    g = base + (b - 2)
                    dve.wait_ge(out_psum, g + 1)
                    v.tensor_copy(tiles_of(s.Xv, g)[:, :, 0:C],
                                  s.bank(OUT + b % 2).rearrange("p (t f) -> p t f", t=GRP)[:, :, C:2 * C]).then_inc(dst_ready, 1)
            pipeline(dve, tick, 2)

        @block.scalar
        def _(act):
            def tick(base, b):
                if group_live(base, b, 0):
                    g = base + b
                    act.wait_ge(xT_psum, g + 1)
                    wait(act, out_psum, g - 1)
                    nc.scalar.copy(xT[0:C, b % 2], s.bank(TURN + b % 2)[0:C, :]).then_inc(xT_ready, 1)
                if group_live(base, b, 2):
                    g = base + (b - 2)
                    act.wait_ge(dst_ready, g + 1)
                    nc.scalar.copy(tiles_of(by_src, g),
                                   s.bank(OUT + b % 2).rearrange("p (t f) -> p t f", t=GRP)[:, :, 0:C]).then_inc(src_ready, 1)
            pipeline(act, tick, 2)


def pass_pna(nc, s, A):
    wk = Carver(s.work)
    onehot = wk.f32(4 * B4 * P).rearrange("p (r t n) -> p r t n", r=4, t=B4)
    parts = wk.f32(4 * B4 * 5 * C).rearrange("p (r t f) -> p r t f", r=4, t=B4)
    spread = wk.f32(2 * B4 * P).rearrange("p (r t n) -> p r t n", r=2, t=B4)
    running = wk.f32(2 * B4 * P).rearrange("p (r n) -> p r n", r=2)
    resets = wk.bf16(4 * B4 * P).rearrange("p (r n) -> p r n", r=4)
    attrs = wk.f32(2 * P).rearrange("p (r n) -> p r n", r=2)[0:B4 * 4]
    ring = wk.f32(4 * B4 * C).rearrange("p (r t f) -> p r t f", r=4, t=B4)
    u_sum = wk.f32(B4 * C).rearrange("p (t f) -> p t f", t=B4)
    slots = wk.i32(ROUND * B4).rearrange("p (r t) -> p r t", r=ROUND)
    sums = s.arena[:, :]
    W4 = 4 * C
    names = ("rows_ready", "onehot_ready", "onehot_turned", "spread_ready", "u_psum", "u_summed", "u_ready",
             "negated", "squared", "u_turned", "maxima_ready", "maxima_turned", "maxima_back", "part_ready",
             "added", "released")
    (rows_ready, onehot_ready, onehot_turned, spread_ready, u_psum, u_summed, u_ready, negated, squared, u_turned,
     maxima_ready, maxima_turned, maxima_back, part_ready, added, released) = (s.sem("pna_" + n) for n in names)
    released_loads = s.sem("pna_released_loads")
    landed = [s.sem(f"pna_landed{k}") for k in range(4)]
    resets_landed = [s.sem(f"pna_resets_landed{k}") for k in range(4)]
    attrs_landed = [s.sem(f"pna_attrs_landed{k}") for k in range(2)]
    SPREAD, MESSAGE, TURN, BACK, PART = 0, 1, 2, 3, 4

    def loads(base, b, r):
        return base * (16 // r) + (b // r + 1) * 16

    with nc.Block() as block:
        @block.gpsimd
        def _(pool):
            gather_rows(pool, s, s.message_table, lambda r, i: ring[:, r, i, :], slots, landed, rows_ready, u_summed, released)

        @block.sync
        def _(sp):
            def tick(base, b):
                q = base + b
                wait(sp, u_psum, q - 1)
                sp.dma_start(attrs[:, b % 2, :], s.attr_rows[bass.ds(q * (B4 * 4), B4 * 4), :]).then_inc(attrs_landed[b % 2], 16)
                wait(sp, maxima_ready, q - 3)
                sp.sem_inc(released_loads, 1)
                sp.dma_start(resets[:, b % 4, :], s.reset_rows[bass.ds(q * (B4 * P), B4 * P)].partition_broadcast(P))\
                    .then_inc(resets_landed[b % 4], 16)
            rounds(sp, tick, 0)
            for k in range(2):
                sp.wait_ge(attrs_landed[k], 8 * NB)
            for k in range(4):
                sp.wait_ge(resets_landed[k], 4 * NB)

        @block.tensor
        def _(pe):
            js = [pe.alloc_register(f"pna_pe_tile{i}") for i in range(B4)]

            def tick(base, b):
                if live(base, b, 1):
                    pe.load(js, s.node_tile[0:1, steps4(base, b, 1)])
                    tiles = [pe.snap(pe.snap(j, min_val=0, max_val=NT - 1) * C1) for j in js]
                if live(base, b, 4):
                    q = base + (b - 4)
                    pe.wait_ge(maxima_back, q + 1)
                    pe.wait_ge(squared, q + 1)
                    wait(pe, added, B4 * q)
                    for i in range(B4):
                        m = nc.tensor.matmul(s.bank(PART + b % 2 * 2, 2)[:, i * W4:(i + 1) * W4], onehot[:, (b - 4) % 4, i, :],
                                             parts[:, (b - 4) % 4, i, C:5 * C], start=True, stop=True)
                    m.then_inc(part_ready, 1)
                if live(base, b, 3):
                    q = base + (b - 3)
                    pe.wait_ge(maxima_ready, q + 1)
                    wait(pe, maxima_back, q)
                    for i in range(B4):
                        m = nc.tensor.transpose(s.bank(BACK)[:, i * P:(i + 1) * P], running[:, (b - 3) % 2, i * P:(i + 1) * P], s.ident[:, :])
                    m.then_inc(maxima_turned, 1)
                if live(base, b, 1):
                    q = base + (b - 1)
                    pe.wait_ge(attrs_landed[(b - 1) % 2], loads(base, b - 1, 2))
                    pe.wait_ge(spread_ready, q + 1)
                    wait(pe, u_summed, q)
                    nc.tensor.matmul(s.bank(MESSAGE)[:, 0:B4 * C], attrs[:, (b - 1) % 2, :], s.attr_weight[:, :], start=True, stop=False)
                    for i in range(B4):
                        m = nc.tensor.matmul(s.bank(MESSAGE)[:, i * C:(i + 1) * C], spread[:, (b - 1) % 2, i, :],
                                             s.X[:, bass.ds(tiles[i], C)], start=False, stop=i == B4 - 1)
                    m.then_inc(u_psum, 1)
                if live(base, b, 2):
                    q = base + (b - 2)
                    pe.wait_ge(negated, q + 1)
                    wait(pe, maxima_ready, q)
                    for i in range(B4):
                        m = nc.tensor.transpose(s.bank(TURN)[:, i * P:(i + 1) * P], parts[:, (b - 2) % 4, i, 0:2 * C], s.ident[:, :])
                    m.then_inc(u_turned, 1)
                if live(base, b, 0):
                    q = base + b
                    pe.wait_ge(onehot_ready, q + 1)
                    wait(pe, spread_ready, q)
                    for i in range(B4):
                        m = nc.tensor.transpose(s.bank(SPREAD)[:, i * P:(i + 1) * P], onehot[:, b % 4, i, :], s.ident[:, :])
                    m.then_inc(onehot_turned, 1)
            rounds(pe, tick, 4)

        @block.scalar
        def _(act):
            def tick(base, b):
                if live(base, b, 3):
                    q = base + (b - 3)
                    act.wait_ge(maxima_turned, q + 1)
                    for i in range(B4):
                        m = nc.scalar.activation(parts[:, (b - 3) % 4, i, 3 * C:5 * C], s.bank(BACK)[:, i * P:(i + 1) * P], ACT.Copy,
                                                 scale=s.last_col[:, bass.ds(q * B4 + i, 1)])
                    m.then_inc(maxima_back, 1)
                u = parts[:, (b - 1) % 4, :, C:2 * C]
                if live(base, b, 1):
                    act.wait_ge(u_ready, base + b)
                    nc.scalar.mul(parts[:, (b - 1) % 4, :, 0:C], u, -1.0).then_inc(negated, 1)
                if live(base, b, 0):
                    act.wait_ge(onehot_turned, base + (b + 1))
                    wait(act, u_psum, base + (b - 1))
                    nc.scalar.copy(spread[:, b % 2], s.bank(SPREAD).rearrange("p (t n) -> p t n", t=B4)).then_inc(spread_ready, 1)
                if live(base, b, 1):
                    nc.scalar.square(parts[:, (b - 1) % 4, :, 2 * C:3 * C], u).then_inc(squared, 1)
            rounds(act, tick, 3)

        @block.vector
        def _(dve):
            v = nc.vector
            for k in range(B4):
                v.memset(sums[:, k * (NTP * C):(k + 1) * (NTP * C)], 0.0).then_inc(added, 1)
            v.memset(running[:, 1, :], NEG)
            js = [dve.alloc_register(f"pna_tile{i}") for i in range(B4)]
            LAG = 4

            def tick(base, b):
                if live(base, b, 0):
                    wait(dve, u_psum, base + (b - 7))
                    v.tensor_copy(slots[:, b, :], s.message_row[:, steps4(base, b)]).then_inc(rows_ready, 1)
                if live(base, b, LAG):
                    wait(dve, part_ready, base + (b - LAG - 3))
                    v.tensor_tensor(onehot[:, b % 4], s.iota_row[:, :].unsqueeze(1).broadcast_to((P, B4, P)),
                                    s.rel_col[:, steps4(base, b, LAG)].unsqueeze(2).broadcast_to((P, B4, P)),
                                    ALU.is_equal).then_inc(onehot_ready, 1)
                lag = LAG + 4
                if live(base, b, lag):
                    qa = base + (b - lag)
                    dve.load(js, s.node_tile[0:1, steps4(base, b, lag)])
                    tiles = [dve.snap(dve.snap(j, min_val=0, max_val=NT - 1) * W4) for j in js]
                    dve.wait_ge(part_ready, qa + 1)

                def add(i):
                    if live(base, b, LAG + 4):
                        dve.wait_ge(added, qa * B4 + (B4 + i))
                        to = sums[:, bass.ds(tiles[i], W4)]
                        v.tensor_tensor(to, s.bank(PART + b % 2 * 2, 2)[:, i * W4:(i + 1) * W4], to, ALU.add).then_inc(added, 1)

                add(0)
                if live(base, b, LAG + 1):
                    r = b - LAG - 1
                    q = base + r
                    dve.wait_ge(landed[r % 4], landings(base, r))
                    dve.wait_ge(u_psum, q + 1)
                    wait(dve, u_ready, q)
                    v.tensor_tensor(u_sum, s.bank(MESSAGE)[:, 0:B4 * C].rearrange("p (t f) -> p t f", t=B4), ring[:, r % 4],
                                    ALU.add).then_inc(u_summed, 1)
                add(1)
                if live(base, b, LAG + 1):
                    dve.wait_ge(u_summed, q + 1)
                    v.tensor_tensor(parts[:, r % 4, :, C:2 * C], u_sum,
                                    s.ew_col[:, steps4(base, b, LAG + 1)].unsqueeze(2).broadcast_to((P, B4, C)),
                                    ALU.mult).then_inc(u_ready, 1)
                add(2)
                if live(base, b, LAG + 2):
                    r2 = b - LAG - 2
                    q2 = base + r2
                    dve.wait_ge(u_turned, q2 + 1)
                    dve.wait_ge(resets_landed[r2 % 4], loads(base, r2, 4))
                    wait(dve, maxima_turned, q2 - 1)
                    wait(dve, maxima_ready, q2)
                    v.tensor_tensor_scan(running[:, r2 % 2, :], resets[:, r2 % 4, :], s.bank(TURN),
                                         running[:, (r2 + 1) % 2, B4 * P - 1:B4 * P], ALU.add, ALU.max).then_inc(maxima_ready, 1)
                add(3)
            rounds(dve, tick, LAG + 4)


def node_pna_out(nc, s, A):
    sums = s.arena[:, :].rearrange("p (j f) -> p j f", f=4 * C)
    wk = Carver(s.work)
    Wagg = wk.f32(2 * 3 * C).rearrange("p (k f) -> p k f", k=2)
    W, Wm, Wx = wk.f32(C)[0:C, :], wk.f32(C)[0:C, :], wk.f32(C)[0:C1, :]
    WT, bpre = wk.f32(C)[0:C, :], wk.f32(C)
    scale_n, has, deg, logd, s2, s3 = (wk.f32(NTP) for _ in range(6))
    vec, logs, log_sum, avg, avg_inv = wk.f32(NTP), wk.f32(NTP), wk.f32(1), wk.f32(1), wk.f32(1)
    ones_col = wk.f32(P)
    agg = wk.f32(2 * GRP * 4 * C).rearrange("p (r t f) -> p r t f", r=2, t=GRP)
    squares_ring, shift_ring = (wk.f32(2 * GRP * C).rearrange("p (r t f) -> p r t f", r=2, t=GRP) for _ in range(2))
    x = wk.f32(2 * GRP * C1).rearrange("p (r t f) -> p r t f", r=2, t=GRP)
    aggT0, aggT1, xT = (wk.f32(2 * GRP * P).rearrange("p (r n) -> p r n", r=2) for _ in range(3))
    scaled2, scaled3 = (wk.f32(2 * GRP * C).rearrange("p (r t f) -> p r t f", r=2, t=GRP) for _ in range(2))
    names = ("loaded", "x_loaded", "scalars", "logs_ready", "mean_log", "W_turned", "W_ready", "Wx_psum", "Wx_ready",
             "work", "agg_ready", "x_ready", "deviation", "turned", "agg_turned", "out_psum", "out_ready", "combine",
             "variance")
    (loaded, x_loaded, scalars, logs_ready, mean_log, W_turned, W_ready, Wx_psum, Wx_ready,
     work, agg_ready, x_ready, deviation, turned, agg_turned, out_psum, out_ready, combine,
     variance) = (s.sem("pna_out_" + n) for n in names)
    TURN, OUT, SMALL = 0, 3, 7
    NV = N // NTP
    over = lambda t: t.unsqueeze(2).broadcast_to((P, GRP, C))
    group_col = lambda t, g: t[:, bass.ds(g * GRP, GRP)]
    cols = lambda t: t.rearrange("p (t f) -> p t f", t=GRP)
    n_loaded = 9 + 6

    with nc.Block() as block:
        @block.sync
        def _(sp):
            sp.dma_start(s.X[:, :], s.x_saved).then_inc(x_loaded, 16)
            for k in range(3):
                at = C + 4 * C * k
                to = slice(k * C, (k + 1) * C)
                sp.dma_start(Wagg[0:C, 0, to], A["L1_gnn_Wpost"][at:at + C, :]).then_inc(loaded, 16)
                sp.dma_start(Wagg[C:P, 0, to], A["L1_gnn_Wpost"][at + 3 * C:at + 4 * C, :]).then_inc(loaded, 16)
                sp.dma_start(Wagg[:, 1, to], A["L1_gnn_Wpost"][at + C:at + 3 * C, :]).then_inc(loaded, 16)
            sp.dma_start(W, A["L1_gnn_W"]).then_inc(loaded, 16)
            sp.dma_start(Wm, A["L1_gnn_Wpost"][0:C, :]).then_inc(loaded, 16)
            sp.dma_start(Wx[C:C1, :], A["L1_gnn_bpost"].unsqueeze(0)).then_inc(loaded, 16)
            sp.dma_start(bpre, A["L1_gnn_bpre"].partition_broadcast(P)).then_inc(loaded, 16)
            sp.dma_start(vec[0:NV, :], A["node_vec"].rearrange("(p j) -> p j", p=NV)).then_inc(loaded, 16)
            sp.dma_start(vec[NV:P, :], A["node_vec"][0:(P - NV) * NTP].rearrange("(p j) -> p j", p=P - NV)).then_inc(loaded, 16)
            sp.wait_ge(loaded, 16 * n_loaded)

        @block.vector
        def _(dve):
            v = nc.vector
            done = chain(dve, scalars)
            v.memset(ones_col, 1.0)
            v.tensor_scalar(has, s.count[:, :], 1.0, None, ALU.min)
            done(v.tensor_scalar(deg, s.count[:, :], 1.0, None, ALU.max))
            done(v.reciprocal(scale_n, deg))
            dve.wait_ge(loaded, 16 * n_loaded)
            dve.wait_ge(x_loaded, 16)
            dve.wait_ge(W_turned, 1)
            v.tensor_copy(WT, s.bank(SMALL)[0:C, 0:C]).then_inc(W_ready, 1)
            dve.wait_ge(Wx_psum, 1)
            v.tensor_copy(Wx[0:C, :], s.bank(SMALL)[0:C, 0:C]).then_inc(Wx_ready, 1)
            dve.wait_ge(mean_log, 1)
            done(v.tensor_scalar(avg, s.bank(SMALL)[:, C:C + 1], 1.0 / N, None, ALU.mult))
            done(v.reciprocal(avg_inv, avg))
            done(v.reciprocal(s3, logd))
            v.tensor_scalar(s2, logd, avg_inv[:, 0:1], None, ALU.mult)
            done(v.tensor_scalar(s3, s3, avg[:, 0:1], None, ALU.mult))
            done(v.tensor_tensor(s3, s3, s2, ALU.mult))

            def tick(base, b):
                if group_live(base, b, 0):
                    g = base + b
                    a, squares, shift = agg[:, b % 2], squares_ring[:, b % 2], shift_ring[:, b % 2]
                    wait(dve, turned, g - 1)
                    v.tensor_tensor(a[:, :, 0:2 * C], tiles_of(sums, g)[:, :, 0:2 * C],
                                    group_col(scale_n, g).unsqueeze(2).broadcast_to((P, GRP, 2 * C)), ALU.mult).then_inc(work, 1)
                    v.tensor_tensor(shift, over(group_col(has, g)), bpre.unsqueeze(1).broadcast_to((P, GRP, C)), ALU.mult).then_inc(work, 1)
                    dve.wait_ge(work, g * 3 + 1)
                    v.tensor_tensor(squares, a[:, :, 0:C], a[:, :, 0:C], ALU.mult).then_inc(work, 1)
                if group_live(base, b, 3):
                    g3 = base + (b - 3)
                    dve.wait_ge(out_psum, g3 + 1)
                    o1, o2 = scaled2[:, (b - 3) % 2], scaled3[:, (b - 3) % 2]
                    out4 = s.bank(OUT + (b - 3) % 2 * 2, 2).rearrange("p (t f) -> p t f", t=GRP)
                    v.tensor_tensor(o1, out4[:, :, C:2 * C], over(group_col(s2, g3)), ALU.mult)
                    v.tensor_tensor(o2, out4[:, :, 2 * C:3 * C], over(group_col(s3, g3)), ALU.mult).then_inc(combine, 1)
                if group_live(base, b, 0):
                    dve.wait_ge(work, g * 3 + 3)
                    v.tensor_tensor(a[:, :, C:2 * C], a[:, :, C:2 * C], squares, ALU.subtract).then_inc(variance, 1)
                if group_live(base, b, 3):
                    dve.wait_ge(combine, g3 * 2 + 1)
                    v.tensor_tensor(o1, o1, o2, ALU.add).then_inc(combine, 1)
                if group_live(base, b, 0):
                    v.tensor_tensor(a[:, :, 0:C], a[:, :, 0:C], shift, ALU.add)
                    v.tensor_tensor(a[:, :, 2 * C:3 * C], shift, tiles_of(sums, g)[:, :, 2 * C:3 * C], ALU.subtract)
                    v.tensor_tensor(a[:, :, 3 * C:4 * C], shift, tiles_of(sums, g)[:, :, 3 * C:4 * C], ALU.add).then_inc(agg_ready, 1)
                if group_live(base, b, 3):
                    dve.wait_ge(combine, g3 * 2 + 2)
                    v.tensor_tensor(tiles_of(sums, g3)[:, :, 0:C], out4[:, :, 0:C], o1, ALU.add).then_inc(out_ready, 1)
            pipeline(dve, tick, 3)

        @block.scalar
        def _(act):
            act.wait_ge(loaded, 16 * n_loaded)
            act.wait_ge(x_loaded, 16)
            nc.scalar.activation(logs[0:NV, :], vec[0:NV, :], ACT.Ln, bias=1.0, accum_out=log_sum[0:NV, :]).then_inc(logs_ready, 1)
            act.wait_ge(scalars, 1)
            nc.scalar.activation(logd, deg, ACT.Ln, bias=1.0).then_inc(logs_ready, 1)

            def tick(base, b):
                if group_live(base, b, 0):
                    wait(act, turned, base + (b - 1))
                    nc.scalar.copy(x[:, b % 2], tiles_of(s.Xv, base + b)).then_inc(x_ready, 1)
                if group_live(base, b, 1):
                    r = (b - 1) % 2
                    act.wait_ge(turned, base + b)
                    wait(act, out_psum, base + (b - 2))
                    nc.scalar.copy(xT[0:C1, r], s.bank(TURN + 2)[0:C1, :])
                    nc.scalar.copy(aggT0[:, r], s.bank(TURN))
                    nc.scalar.copy(aggT1[:, r], s.bank(TURN + 1)).then_inc(agg_turned, 1)
                if group_live(base, b, 0):
                    g = base + b
                    std = agg[:, b % 2, :, C:2 * C]
                    act.wait_ge(variance, g + 1)
                    nc.scalar.activation(std, std, ACT.Relu).then_inc(deviation, 1)
                    act.wait_ge(deviation, g * 2 + 1)
                    nc.scalar.activation(std, std, ACT.Sqrt, bias=s.eps_col[:, 0:1]).then_inc(deviation, 1)
            pipeline(act, tick, 1)

        @block.tensor
        def _(pe):
            t_ = nc.tensor
            pe.wait_ge(loaded, 16 * n_loaded)
            t_.transpose(s.bank(SMALL)[0:C, 0:C], W, s.ident[0:C, 0:C]).then_inc(W_turned, 1)
            pe.wait_ge(W_ready, 1)
            t_.matmul(s.bank(SMALL)[0:C, 0:C], WT, Wm, start=True, stop=True).then_inc(Wx_psum, 1)
            pe.wait_ge(Wx_ready, 1)
            pe.wait_ge(logs_ready, 2)
            t_.matmul(s.bank(SMALL)[:, C:C + 1], ones_col[0:NV, :], log_sum[0:NV, :], start=True, stop=True).then_inc(mean_log, 1)

            def tick(base, b):
                if group_live(base, b, 0):
                    g, r = base + b, b % 2
                    pe.wait_ge(agg_ready, g + 1)
                    pe.wait_ge(x_ready, g + 1)
                    pe.wait_ge(deviation, g * 2 + 2)
                    wait(pe, agg_turned, g)
                    turn_group(nc, s, agg[:, r, :, 0:P], s.bank(TURN), P)
                    turn_group(nc, s, agg[:, r, :, P:2 * P], s.bank(TURN + 1), P)
                    turn_group(nc, s, x[:, r], s.bank(TURN + 2), C1).then_inc(turned, 1)
                if group_live(base, b, 1):
                    g, r = base + (b - 1), (b - 1) % 2
                    pe.wait_ge(agg_turned, g + 1)
                    wait(pe, out_ready, g - 1)
                    for t in range(GRP):
                        to, at = s.bank(OUT + r * 2, 2)[:, t * 4 * C:t * 4 * C + 3 * C], slice(t * P, (t + 1) * P)
                        t_.matmul(to, aggT0[:, r, at], Wagg[:, 0, :], start=True, stop=False)
                        t_.matmul(to, aggT1[:, r, at], Wagg[:, 1, :], start=False, stop=False)
                        m = t_.matmul(to[:, 0:C], xT[0:C1, r, at], Wx, start=False, stop=True)
                    m.then_inc(out_psum, 1)
            pipeline(pe, tick, 1)


def node_pna_gru(nc, s, A):
    sums = s.arena[:, :].rearrange("p (j f) -> p j f", f=4 * C)
    y, square = sums[:, :, C:2 * C], sums[:, :, 2 * C:3 * C]
    wk = Carver(s.work)
    Wih, Whh = wk.f32(3 * C)[0:C1, :], wk.f32(4 * C)[0:C1, :]
    o, x = (wk.f32(2 * GRP * C1).rearrange("p (r t f) -> p r t f", r=2, t=GRP) for _ in range(2))
    oT, xT = (wk.f32(2 * GRP * P).rearrange("p (r n) -> p r n", r=2) for _ in range(2))
    rz = wk.f32(2 * GRP * 2 * C).rearrange("p (r t f) -> p r t f", r=2, t=GRP)
    new, diff = (wk.f32(2 * GRP * C).rearrange("p (r t f) -> p r t f", r=2, t=GRP) for _ in range(2))
    names = ("loaded", "ones", "inputs_ready", "turned", "turned_back", "gates_psum", "gates_ready", "new_steps",
             "new_sum", "new_ready", "y_ready", "mix")
    (loaded, ones, inputs_ready, turned, turned_back, gates_psum, gates_ready, new_steps,
     new_sum, new_ready, y_ready, mix) = (s.sem("gru_" + n) for n in names)
    TURN, GATES = 0, 2
    gates = [s.bank(GATES + 2 * r, 2).rearrange("p (t f) -> p t f", t=GRP) for r in range(2)]

    with nc.Block() as block:
        @block.sync
        def _(sp):
            sp.dma_start(Wih[0:C, :], A["L1_gnn_Wih"]).then_inc(loaded, 16)
            sp.dma_start(Wih[C:C1, :], A["L1_gnn_bih"].unsqueeze(0)).then_inc(loaded, 16)
            for to, of in ((slice(0, 2 * C), slice(0, 2 * C)), (slice(3 * C, 4 * C), slice(2 * C, 3 * C))):
                sp.dma_start(Whh[0:C, to], A["L1_gnn_Whh"][:, of]).then_inc(loaded, 16)
                sp.dma_start(Whh[C:C1, to], A["L1_gnn_bhh"][of].unsqueeze(0)).then_inc(loaded, 16)
            sp.wait_ge(loaded, 96)

        @block.vector
        def _(dve):
            v = nc.vector
            v.memset(Whh[:, 2 * C:3 * C], 0.0)
            v.memset(o[:, :, :, C:C1], 1.0).then_inc(ones, 1)

            def tick(base, b):
                if group_live(base, b, 0):
                    g = base + b
                    wait(dve, turned, g - 1)
                    v.tensor_copy(o[:, b % 2, :, 0:C], tiles_of(sums, g)[:, :, 0:C])
                    v.tensor_copy(x[:, b % 2], tiles_of(s.Xv, g)).then_inc(inputs_ready, 1)
                if group_live(base, b, 3):
                    q3, r3 = base + (b - 3), (b - 3) % 2
                    dve.wait_ge(new_ready, q3 + 1)
                    xs = tiles_of(s.Xv, q3)[:, :, 0:C]
                    v.tensor_tensor(diff[:, r3], xs, new[:, r3], ALU.subtract).then_inc(mix, 1)
                if group_live(base, b, 2):
                    q2, r2 = base + (b - 2), b % 2
                    dve.wait_ge(gates_ready, q2 + 1)
                    v.tensor_tensor(new[:, r2], rz[:, r2, :, 0:C], gates[r2][:, :, 3 * C:4 * C], ALU.mult).then_inc(new_steps, 1)
                if group_live(base, b, 3):
                    dve.wait_ge(mix, q3 * 3 + 1)
                    v.tensor_tensor(diff[:, r3], diff[:, r3], rz[:, r3, :, C:2 * C], ALU.mult).then_inc(mix, 1)
                    v.tensor_tensor(new[:, r3], new[:, r3], xs, ALU.add).then_inc(mix, 1)
                if group_live(base, b, 2):
                    dve.wait_ge(new_steps, q2 + 1)
                    v.tensor_tensor(new[:, r2], new[:, r2], gates[r2][:, :, 2 * C:3 * C], ALU.add).then_inc(new_sum, 1)
                if group_live(base, b, 3):
                    dve.wait_ge(mix, q3 * 3 + 3)
                    v.tensor_tensor(tiles_of(y, q3), new[:, r3], diff[:, r3], ALU.add).then_inc(y_ready, 1)
            pipeline(dve, tick, 3)

        @block.scalar
        def _(act):
            def tick(base, b):
                if group_live(base, b, 0):
                    r = b % 2
                    act.wait_ge(turned, base + (b + 1))
                    wait(act, gates_psum, base + (b - 1))
                    nc.scalar.copy(oT[0:C1, r], s.bank(TURN)[0:C1, :])
                    nc.scalar.copy(xT[0:C1, r], s.bank(TURN + 1)[0:C1, :]).then_inc(turned_back, 1)
                if group_live(base, b, 1):
                    q, r = base + (b - 1), (b - 1) % 2
                    act.wait_ge(gates_psum, q + 1)
                    wait(act, y_ready, q - 1)
                    nc.scalar.activation(rz[:, r], gates[r][:, :, 0:2 * C], ACT.Sigmoid).then_inc(gates_ready, 1)
                if group_live(base, b, 2):
                    r = b % 2
                    act.wait_ge(new_sum, base + (b - 1))
                    nc.scalar.activation(new[:, r], new[:, r], ACT.Tanh).then_inc(new_ready, 1)
            pipeline(act, tick, 2)

        @block.tensor
        def _(pe):
            t_ = nc.tensor
            pe.wait_ge(loaded, 96)
            pe.wait_ge(ones, 1)

            def tick(base, b):
                if group_live(base, b, 0):
                    g, r = base + b, b % 2
                    pe.wait_ge(inputs_ready, g + 1)
                    wait(pe, turned_back, g)
                    turn_group(nc, s, o[:, r], s.bank(TURN), C1)
                    turn_group(nc, s, x[:, r], s.bank(TURN + 1), C1).then_inc(turned, 1)
                if group_live(base, b, 1):
                    g, r = base + (b - 1), (b - 1) % 2
                    pe.wait_ge(turned_back, g + 1)
                    wait(pe, new_sum, g - 1)
                    for t in range(GRP):
                        to, at = s.bank(GATES + 2 * r, 2)[:, t * 4 * C:(t + 1) * 4 * C], slice(t * P, (t + 1) * P)
                        t_.matmul(to, xT[0:C1, r, at], Whh, start=True, stop=False)
                        m = t_.matmul(to[:, 0:3 * C], oT[0:C1, r, at], Wih, start=False, stop=True)
                    m.then_inc(gates_psum, 1)
            pipeline(pe, tick, 1)
    layer_norm(nc, s, "pna_norm", y, square, s.Xv[:, :, 0:C])


def pass_scatter(nc, s, layer):
    tables = s.tables[layer]
    columns = s.arena[:, 0:3 * STEPS]
    target_col, weight_col = columns[:, 0:STEPS], columns[:, STEPS:2 * STEPS]
    scatter_row = columns[:, 2 * STEPS:3 * STEPS].bitcast(I32)
    wk = Carver(s.work)
    spread = wk.f32(2 * B4 * P).rearrange("p (r t n) -> p r t n", r=2, t=B4)
    same = wk.f32(4 * B4 * P).rearrange("p (r t n) -> p r t n", r=4, t=B4)
    weighted = wk.f32(2 * B4 * F).rearrange("p (r t f) -> p r t f", r=2, t=B4)
    merged = wk.f32(4 * B4 * F).rearrange("p (r t f) -> p r t f", r=4, t=B4)
    rels, targets = (wk.f32(ROUND * B4).rearrange("p (r t) -> p r t", r=ROUND) for _ in range(2))
    slots = wk.i32(ROUND * B4).rearrange("p (r t) -> p r t", r=ROUND)
    names = ("loaded", "released", "copied", "rels_turned", "targets_turned", "spread_ready", "same_ready", "x_psum",
             "weighted_ready", "merged_psum", "merged_ready", "rows_ready")
    (loaded, released, copied, rels_turned, targets_turned, spread_ready, same_ready, x_psum,
     weighted_ready, merged_psum, merged_ready, rows_ready) = (s.sem(f"scatter{layer}_{n}") for n in names)
    scattered = [s.sem(f"scatter{layer}_done{k}") for k in range(K)]
    REL, TARGET, X_BANK, MERGED = 0, 1, 2, 4
    CYCLE = K // B4

    def scatters(base, b):
        return (base + b) // CYCLE * 16 if isinstance(base, int) else base * (16 // CYCLE) + b // CYCLE * 16

    with nc.Block() as block:
        @block.sync
        def _(sp):
            sp.dma_start(columns, s.saved_cols).then_inc(loaded, 16)
            sp.wait_ge(loaded, 16)

        @block.gpsimd
        def _(pool):
            def tick(base, b):
                q = base + b
                pool.wait_ge(rows_ready, q + 1)
                pool.wait_ge(merged_ready, q + 1)
                for i in range(B4):
                    k = b % CYCLE * B4 + i
                    wait(pool, scattered[k], scatters(base, b))
                    pool.sem_inc(released, 1)
                    pool.indirect_dma_start(tables[k], bass.IndirectOffsetOnAxis(ap=slots[:, b, i:i + 1], axis=0),
                                            merged[:, b % 4, i, :], None, compute_op=ALU.add).then_inc(scattered[k], 16)
            rounds(pool, tick, 0)
            for k in range(K):
                pool.wait_ge(scattered[k], 16 * NB // CYCLE)

        @block.scalar
        def _(act):
            act.wait_ge(loaded, 16)

            def tick(base, b):
                if live(base, b, 0):
                    wait(act, same_ready, base + (b - 7))
                    nc.scalar.copy(rels[:, b, :], s.rel_col[:, steps4(base, b)])
                    nc.scalar.copy(targets[:, b, :], target_col[:, steps4(base, b)]).then_inc(copied, 1)
                if live(base, b, 4):
                    act.wait_ge(merged_psum, base + (b - 3))
                    for i in range(B4):
                        wait(act, scattered[b % CYCLE * B4 + i], scatters(base, b - 8 + CYCLE))
                    nc.scalar.copy(merged[:, b % 4], s.bank(MERGED + b % 2)[:, 0:B4 * F].rearrange("p (t f) -> p t f", t=B4))\
                        .then_inc(merged_ready, 1)
            rounds(act, tick, 4)

        @block.tensor
        def _(pe):
            js = [pe.alloc_register(f"scatter{layer}_tile{i}") for i in range(B4)]

            def tick(base, b):
                if live(base, b, 4):
                    q = base + (b - 4)
                    pe.wait_ge(weighted_ready, q + 1)
                    wait(pe, merged_ready, q - 1)
                    for i in range(B4):
                        m = nc.tensor.matmul(s.bank(MERGED + b % 2)[:, i * F:(i + 1) * F], same[:, b % 4, i, :],
                                             weighted[:, b % 2, i, :], start=True, stop=True)
                    m.then_inc(merged_psum, 1)
                if live(base, b, 2):
                    q = base + (b - 2)
                    pe.load(js, s.node_tile[0:1, steps4(base, b, 2)])
                    tiles = [pe.snap(pe.snap(j, min_val=0, max_val=NT - 1) * C1) for j in js]
                    pe.wait_ge(spread_ready, q + 1)
                    wait(pe, weighted_ready, q - 1)
                    for i in range(B4):
                        m = nc.tensor.matmul(s.bank(X_BANK + b % 2)[:, i * C1:(i + 1) * C1], spread[:, b % 2, i, :],
                                             s.X[:, bass.ds(tiles[i], C1)], start=True, stop=True)
                    m.then_inc(x_psum, 1)
                if live(base, b, 1):
                    q = base + (b - 1)
                    pe.wait_ge(copied, q + 1)
                    wait(pe, spread_ready, q)
                    for i in range(B4):
                        m = nc.tensor.transpose(s.bank(REL)[:, i * P:(i + 1) * P],
                                                rels[:, (b - 1) % ROUND, i:i + 1].broadcast_to((P, P)), s.ident[:, :])
                    m.then_inc(rels_turned, 1)
                    wait(pe, same_ready, q)
                    for i in range(B4):
                        m = nc.tensor.transpose(s.bank(TARGET)[:, i * P:(i + 1) * P],
                                                targets[:, (b - 1) % ROUND, i:i + 1].broadcast_to((P, P)), s.ident[:, :])
                    m.then_inc(targets_turned, 1)
            rounds(pe, tick, 4)

        @block.vector
        def _(dve):
            v = nc.vector
            v.memset(weighted[:, :, :, C1:F], 1.0)
            dve.wait_ge(loaded, 16)

            def tick(base, b):
                if live(base, b, 3):
                    q = base + (b - 3)
                    dve.wait_ge(x_psum, q + 1)
                    wait(dve, merged_psum, q - 1)
                    v.tensor_tensor(weighted[:, (b - 3) % 2, :, 0:C1],
                                    s.bank(X_BANK + (b - 3) % 2)[:, 0:B4 * C1].rearrange("p (t f) -> p t f", t=B4),
                                    weight_col[:, steps4(base, b, 3)].unsqueeze(2).broadcast_to((P, B4, C1)),
                                    ALU.mult).then_inc(weighted_ready, 1)
                if live(base, b, 1):
                    q = base + (b - 1)
                    dve.wait_ge(rels_turned, q + 1)
                    wait(dve, x_psum, q - 1)
                    v.tensor_scalar(spread[:, (b - 1) % 2], s.bank(REL).rearrange("p (t n) -> p t n", t=B4),
                                    s.iota_col[:, 0:1], None, ALU.is_equal).then_inc(spread_ready, 1)
                    dve.wait_ge(targets_turned, q + 1)
                    wait(dve, merged_psum, q - 3)
                    v.tensor_tensor(same[:, (b - 1) % 4], s.bank(TARGET).rearrange("p (t n) -> p t n", t=B4),
                                    targets[:, (b - 1) % ROUND, :].unsqueeze(2).broadcast_to((P, B4, P)),
                                    ALU.is_equal).then_inc(same_ready, 1)
                if live(base, b, 3):
                    wait(dve, merged_ready, base + (b - 6))
                    v.tensor_copy(slots[:, (b - 3) % ROUND, :], scatter_row[:, steps4(base, b, 3)]).then_inc(rows_ready, 1)
            rounds(dve, tick, 4)


def node_scatter(nc, s, A, layer, out=None):
    tables = s.tables[layer]
    K_IN = 2 * C if layer == 0 else C
    R = 2 * C if layer == 0 else F
    M = GRP * F
    ar = Carver(s.arena)
    y, square = (ar.f32(NTP * C).rearrange("p (j f) -> p j f", f=C) for _ in range(2))
    loads = ar.f32(2 * K * 2 * M).rearrange("p (r k m) -> p r k m", r=2, k=K)
    wk = Carver(s.work)
    weight, bias = wk.f32(C)[0:K_IN, :], wk.f32(GRP * C)[0:1, :]
    sums = wk.f32(4 * M).rearrange("p (r t f) -> p r t f", r=4, t=GRP)
    inverse, share = (wk.f32(4 * GRP).rearrange("p (r t) -> p r t", r=4) for _ in range(2))
    rows = wk.f32(4 * GRP * R).rearrange("p (r t f) -> p r t f", r=4, t=GRP)
    rowsT = wk.f32(2 * GRP * P).rearrange("p (r n) -> p r n", r=2)
    names = ("weights_loaded", "summed", "steps", "rows_ready", "rows_turned", "rowsT_ready", "out_psum", "y_ready")
    (weights_loaded, summed, steps, rows_ready, rows_turned, rowsT_ready, out_psum, y_ready) = (
        s.sem(f"node{layer}_{n}") for n in names)
    loaded = [s.sem(f"node{layer}_loaded{r}") for r in range(2)]
    TURN, OUT = 0, 2
    over = lambda t: t.unsqueeze(2).broadcast_to((P, GRP, C))
    LAG = 2 if layer == 0 else 0

    with nc.Block() as block:
        @block.sync
        def _(sp):
            sp.dma_start(weight, A["L2_gnn_weight" if layer == 0 else "L3_gnn_W"]).then_inc(weights_loaded, 16)
            for t in range(GRP):
                sp.dma_start(bias[:, t * C:(t + 1) * C], A["L2_gnn_bias" if layer == 0 else "L3_gnn_b"].unsqueeze(0))\
                    .then_inc(weights_loaded, 16)

            def part(base, b, width=2 * M):
                wait(sp, summed, base + (b - 2))
                for k in range(K):
                    sp.dma_start(loads[:, b // 2 % 2, k, 0:width],
                                 tables[k].rearrange("(p r) f -> p (r f)", p=P)[:, bass.ds((base + b) * M, width)])\
                        .then_inc(loaded[b // 2 % 2], 16)
            part(0, 0)
            part(0, 2)
            with sp.Fori(1, GROUPS // 4) as r:
                part(r * 4, 0)
                part(r * 4, 2)
            part(0, GROUPS - 1, M)
            for r in range(2):
                sp.wait_ge(loaded[r], 16 * K * len(range(2 * r, GROUPS, 4)))
            sp.wait_ge(weights_loaded, 16 * (1 + GRP))

        @block.vector
        def _(dve):
            v = nc.vector

            def tick(base, b):
                if group_live(base, b, 0):
                    g, r = base + b, b % 4
                    to = sums[:, r] if layer == 0 else rows[:, r]
                    dve.wait_ge(loaded[b // 2 % 2], base * (4 * K) + 16 * K * (b // 4 + 1))
                    wait(dve, rows_turned, g - 3)
                    v.tensor_reduce(to.rearrange("p t f -> p (t f)"),
                                    loads[:, b // 2 % 2, :, b % 2 * M:(b % 2 + 1) * M].rearrange("p k m -> p m k"),
                                    AX_X, ALU.add).then_inc(summed, 1)
                if layer == 0 and group_live(base, b, 1):
                    g1, r1 = base + (b - 1), (b - 1) % 4
                    dve.wait_ge(summed, g1 + 1)
                    v.tensor_scalar(inverse[:, r1], sums[:, r1, :, C1], 1.0, None, ALU.max).then_inc(steps, 1)
                if group_live(base, b, LAG + 2):
                    g4 = base + (b - LAG - 2)
                    dve.wait_ge(out_psum, g4 + 1)
                    v.tensor_tensor(tiles_of(y, g4),
                                    s.bank(OUT + (b - LAG - 2) % 2)[:, 0:GRP * C].rearrange("p (t f) -> p t f", t=GRP),
                                    tiles_of(s.Xv, g4)[:, :, 0:C], ALU.add).then_inc(y_ready, 1)
                if layer == 0 and group_live(base, b, 1):
                    dve.wait_ge(steps, g1 * 3 + 1)
                    v.reciprocal(inverse[:, r1], inverse[:, r1]).then_inc(steps, 1)
                if layer == 0 and group_live(base, b, 2):
                    g2, r2 = base + (b - 2), (b - 2) % 4
                    dve.wait_ge(steps, g2 * 3 + 3)
                    v.tensor_tensor(rows[:, r2, :, 0:C], tiles_of(s.Xv, g2)[:, :, 0:C], over(share[:, r2]), ALU.mult)
                if layer == 0 and group_live(base, b, 1):
                    dve.wait_ge(steps, g1 * 3 + 2)
                    v.tensor_tensor(share[:, r1], sums[:, r1, :, C], inverse[:, r1], ALU.mult).then_inc(steps, 1)
                if layer == 0 and group_live(base, b, 2):
                    v.tensor_tensor(rows[:, r2, :, C:2 * C], sums[:, r2, :, 0:C], over(inverse[:, r2]), ALU.mult)\
                        .then_inc(rows_ready, 1)
            pipeline(dve, tick, LAG + 2, 4)

        @block.scalar
        def _(act):
            def tick(base, b):
                if group_live(base, b, 0):
                    g = base + b
                    act.wait_ge(rows_turned, g + 1)
                    wait(act, out_psum, g - 1)
                    nc.scalar.copy(rowsT[0:K_IN, b % 2], s.bank(TURN + b % 2)[0:K_IN, :]).then_inc(rowsT_ready, 1)
            pipeline(act, tick, 0)

        @block.tensor
        def _(pe):
            pe.wait_ge(weights_loaded, 16 * (1 + GRP))
            rows_done = rows_ready if layer == 0 else summed

            def turn(base, b):
                if group_live(base, b, 0):
                    g = base + b
                    pe.wait_ge(rows_done, g + 1)
                    wait(pe, rowsT_ready, g - 1)
                    turn_group(nc, s, rows[:, b % 4], s.bank(TURN + b % 2), R).then_inc(rows_turned, 1)

            def product(base, b):
                if group_live(base, b, 1):
                    g = base + (b - 1)
                    pe.wait_ge(rowsT_ready, g + 1)
                    wait(pe, y_ready, g - 1)
                    to = s.bank(OUT + (b - 1) % 2)
                    nc.tensor.matmul(to[:, 0:GRP * C], s.ones_row[:, :], bias, start=True, stop=False)
                    for t in range(GRP):
                        m = nc.tensor.matmul(to[:, t * C:(t + 1) * C], rowsT[0:K_IN, (b - 1) % 2, t * P:(t + 1) * P], weight,
                                             start=False, stop=t == GRP - 1)
                    m.then_inc(out_psum, 1)

            def tick(base, b):
                if layer == 0:
                    product(base, b)
                turn(base, b)
                if layer == 1:
                    product(base, b)
            pipeline(pe, tick, 1, 4)

    layer_norm(nc, s, f"norm{layer}", y, square, s.Xv[:, :, 0:C], out)


def phases(nc, s, A, out):
    with nc.cleanup_on_exit():
        prepare(nc, s, A)
        pass_gin(nc, s, A)
        node_gin(nc, s, A)
    with nc.cleanup_on_exit():
        messages_pna(nc, s, A)
        pass_pna(nc, s, A)
        node_pna_out(nc, s, A)
        node_pna_gru(nc, s, A)
    for layer in range(2):
        with nc.cleanup_on_exit():
            pass_scatter(nc, s, layer)
            node_scatter(nc, s, A, layer, out if layer == 1 else None)




def build(nc, A, out):
    with ExitStack() as ctx:
        s = Shared()

        def sb(name, shape, dt=F32):
            return ctx.enter_context(nc.sbuf_tensor(name, shape, dt))

        def dram(name, shape, dt=F32):
            return nc.dram_tensor(name, shape, dt, kind="Internal").ap()

        s.sem = lambda name: nc.alloc_semaphore(name=name)
        s.psum = ctx.enter_context(nc.psum_tensor("psum", [P, 8 * 512], F32))
        s.bank = lambda i, n=1: s.psum[:, 512 * i:512 * (i + n)]

        s.edge_rows = dram("edge_rows", (CH * P, NF * P))
        s.reset_rows = dram("reset_rows", (STEPS * P,), BF16)
        s.attr_rows = dram("attr_rows", (STEPS * 4, P))
        s.tile_list = dram("tile_list", (STEPS,), I32)
        s.message_table = dram("message_table", (P * NTP, C))
        s.x_saved = dram("x_saved", (P, NTP * C1))
        s.saved_cols = dram("saved_cols", (P, 3 * STEPS))
        s.tables = [[dram(f"sums{layer}_{k}", (P * NTP, F)) for k in range(K)] for layer in (2, 3)]

        s.X = sb("X", [P, NTP * C1])
        s.Xv = s.X[:, :].rearrange("p (j f) -> p j f", f=C1)
        s.message_row = sb("message_row", [P, STEPS], I32)
        s.rel_col = sb("rel_col", [P, STEPS])
        s.last_col = sb("last_col", [P, STEPS])
        s.ew_col = sb("ew_col", [P, STEPS])
        s.node_tile = sb("node_tile", [1, STEPS], U8)
        s.iota_row = sb("iota_row", [P, P])
        s.ident = sb("ident", [P, P])
        s.iota_col = sb("iota_col", [P, 1])
        s.dummy_col = sb("dummy_col", [P, 1])
        s.one_eps = sb("one_eps", [P, 1])
        s.eps_col = sb("eps_col", [P, 1])
        s.count = sb("count", [P, NTP])
        s.attr_weight = sb("attr_weight", [B4 * 4, B4 * C])
        s.ones_row = sb("ones_row", [1, P])
        s.arena = sb("arena", [P, NTP * 4 * C])
        s.work = sb("work", [P, 12900])

        wk = Carver(s.work)
        s.feature_row = wk.i32(STEPS)
        s.target_col = wk.f32(STEPS)
        s.weight_col = wk.f32(STEPS)
        s.scatter_row = wk.i32(STEPS)
        s.zeros = wk.f32(ZERO)
        s.pass0_at = wk.at
        phases(nc, s, A, out)


def kernel(**inputs):
    import numpy as _np
    import concourse.bacc as _bacc
    from concourse import mybir as _mybir
    from concourse.bass_utils import run_bass_kernel_spmd as _run

    nc = _bacc.Bacc("TRN2", target_bir_lowering=False, num_devices=1)
    arrays, args = {}, {}
    for name in INS:
        a = _np.ascontiguousarray(inputs[name])
        arrays[f"in_{name}_dram"] = a
        args[name] = nc.dram_tensor(f"in_{name}_dram", a.shape, _mybir.dt.from_np(a.dtype), kind="ExternalInput").ap()
    out = nc.dram_tensor("out_0_dram", (N, C), _mybir.dt.float32, kind="ExternalOutput").ap()
    build(nc, args, out)
    return _run(nc, [arrays], core_ids=[0]).results[0]["out_0_dram"]
```
